# Optimizing a Trainium2 kernel written in Bass

```python
import numpy as np
import jax
import jax.numpy as jnp

def _softmax(x, axis=-1):
    return jax.nn.softmax(x, axis=axis)

def _gelu(x):
    return jax.nn.gelu(x, approximate=True)

def _silu(x):
    return jax.nn.silu(x)

def _sigmoid(x):
    return jax.nn.sigmoid(x)

def _layernorm(x, axis=-1, eps=1e-05):
    m = jnp.mean(x, axis=axis, keepdims=True)
    v = jnp.var(x, axis=axis, keepdims=True)
    return (x - m) / jnp.sqrt(v + eps)

def _scatter_add(tgt, idx, src, axis=0):
    return tgt.at[idx].add(src)

def _segment_sum(src, seg, n):
    return jax.ops.segment_sum(src, seg, n)
kernel_name = 'mk_audio_tower_d1_tok_audfeat256_r4_2dc5d3'

def setup_inputs(seed: int=0):
    np.random.seed(seed)
    _w = jnp.asarray

    def _rec_inputs():
        import jax
        import jax.numpy as jnp
        _rk = jax.random.key(seed)
        x = -5.07413e-05 + 0.999912 * jax.random.normal(jax.random.fold_in(_rk, 1), (32, 750, 64), jnp.float32)
        return x
    x = _rec_inputs()

    def _L0_tok_setup():
        import jax, jax.numpy as jnp
        from jax import lax
        import numpy as np
        B, T, C, K, STRIDE = (16, 4000, 64, 5, 2)
        EPS = 0.001
        key = jax.random.key(seed)
        k0, k1, k2, k3 = jax.random.split(key, 4)
        x = jax.random.normal(k0, (B, T, C), dtype=jnp.float32)
        w = jax.random.normal(k1, (K, 1, C), dtype=jnp.float32) * 0.1
        b = jax.random.normal(k2, (C,), dtype=jnp.float32) * 0.01
        gamma = jnp.ones((C,), dtype=jnp.float32)
        beta = jnp.zeros((C,), dtype=jnp.float32)
        alpha = jnp.full((C,), 0.25, dtype=jnp.float32) + 0.01 * jax.random.normal(k3, (C,), dtype=jnp.float32)
        return {'x': x, 'w': w, 'b': b, 'gamma': gamma, 'beta': beta, 'alpha': alpha}
    _L0_tok_all = _L0_tok_setup()
    _L0_tok_in = {k: v for k, v in _L0_tok_all.items() if k in ('w', 'b', 'gamma', 'beta', 'alpha')}
    del _L0_tok_all

    def _L0_attn_setup():
        import math
        import jax, jax.numpy as jnp
        import numpy as np
        EPS_DIV = 1e-07
        EPS_NORM = 1e-12

        def _l2_normalize(x, axis):
            n = jnp.sqrt(jnp.sum(x * x, axis=axis, keepdims=True))
            return x / jnp.maximum(n, EPS_NORM)
        key = jax.random.key(seed)
        ks = jax.random.split(key, 5)
        b, N, C = (8, 1024, 64)
        x = jax.random.normal(ks[0], (b, N, C), dtype=jnp.float32)
        W_qkv = jax.random.normal(ks[1], (C, 3 * C), dtype=jnp.float32) * (1.0 / math.sqrt(C))
        b_qkv = jax.random.normal(ks[2], (3 * C,), dtype=jnp.float32) * 0.02
        W_out = jax.random.normal(ks[3], (C, C), dtype=jnp.float32) * (1.0 / math.sqrt(C))
        b_out = jax.random.normal(ks[4], (C,), dtype=jnp.float32) * 0.02
        return {'x': x, 'W_qkv': W_qkv, 'b_qkv': b_qkv, 'W_out': W_out, 'b_out': b_out}
    _L0_attn_all = _L0_attn_setup()
    _L0_attn_in = {k: v for k, v in _L0_attn_all.items() if k in ('W_qkv', 'b_qkv', 'W_out', 'b_out')}
    del _L0_attn_all

    def _L0_ffn_setup():
        import jax, jax.numpy as jnp
        import numpy as np
        E, D, H, TOP_K = (6, 64, 64, 2)
        ROUTER_H = D // 2
        key = jax.random.key(seed)
        ks = jax.random.split(key, 12)
        s = 1.0 / np.sqrt(D)
        sh = 1.0 / np.sqrt(H)
        sr = 1.0 / np.sqrt(ROUTER_H)
        return {'features': jax.random.normal(ks[0], (8, 1024, D), dtype=jnp.float32), 'router_w1': jax.random.uniform(ks[1], (D, ROUTER_H), jnp.float32, -s, s), 'router_b1': jnp.zeros((ROUTER_H,), jnp.float32), 'router_w2': jax.random.uniform(ks[2], (ROUTER_H, E), jnp.float32, -sr, sr), 'router_b2': jnp.zeros((E,), jnp.float32), 'expert_w1': jax.random.uniform(ks[3], (E, D, H), jnp.float32, -s, s), 'expert_b1': jnp.zeros((E, H), jnp.float32), 'expert_w2': jax.random.uniform(ks[4], (E, H, H), jnp.float32, -sh, sh), 'expert_b2': jnp.zeros((E, H), jnp.float32), 'expert_w3': jax.random.uniform(ks[5], (E, H, D), jnp.float32, -sh, sh), 'expert_b3': jnp.zeros((E, D), jnp.float32)}
    _L0_ffn_all = _L0_ffn_setup()
    _L0_ffn_in = {k: v for k, v in _L0_ffn_all.items() if k in ('router_w1', 'router_b1', 'router_w2', 'router_b2', 'expert_w1', 'expert_b1', 'expert_w2', 'expert_b2', 'expert_w3', 'expert_b3')}
    del _L0_ffn_all
    return {'x': x, 'L0_tok_w': _L0_tok_in['w'], 'L0_tok_b': _L0_tok_in['b'], 'L0_tok_gamma': _L0_tok_in['gamma'], 'L0_tok_beta': _L0_tok_in['beta'], 'L0_tok_alpha': _L0_tok_in['alpha'], 'L0_attn_W_qkv': _L0_attn_in['W_qkv'], 'L0_attn_b_qkv': _L0_attn_in['b_qkv'], 'L0_attn_W_out': _L0_attn_in['W_out'], 'L0_attn_b_out': _L0_attn_in['b_out'], 'L0_ffn_router_w1': _L0_ffn_in['router_w1'], 'L0_ffn_router_b1': _L0_ffn_in['router_b1'], 'L0_ffn_router_w2': _L0_ffn_in['router_w2'], 'L0_ffn_router_b2': _L0_ffn_in['router_b2'], 'L0_ffn_expert_w1': _L0_ffn_in['expert_w1'], 'L0_ffn_expert_b1': _L0_ffn_in['expert_b1'], 'L0_ffn_expert_w2': _L0_ffn_in['expert_w2'], 'L0_ffn_expert_b2': _L0_ffn_in['expert_b2'], 'L0_ffn_expert_w3': _L0_ffn_in['expert_w3'], 'L0_ffn_expert_b3': _L0_ffn_in['expert_b3']}

def reference(x, L0_tok_w, L0_tok_b, L0_tok_gamma, L0_tok_beta, L0_tok_alpha, L0_attn_W_qkv, L0_attn_b_qkv, L0_attn_W_out, L0_attn_b_out, L0_ffn_router_w1, L0_ffn_router_b1, L0_ffn_router_w2, L0_ffn_router_b2, L0_ffn_expert_w1, L0_ffn_expert_b1, L0_ffn_expert_w2, L0_ffn_expert_b2, L0_ffn_expert_w3, L0_ffn_expert_b3):
    import jax
    import jax.numpy as jnp

    def _L0_tok_ref(x, w, b, gamma, beta, alpha):
        import jax, jax.numpy as jnp
        from jax import lax
        import numpy as np
        B, T, C, K, STRIDE = (16, 4000, 64, 5, 2)
        EPS = 0.001
        y = lax.conv_general_dilated(x, w, window_strides=(STRIDE,), padding='SAME', dimension_numbers=('NWC', 'WIO', 'NWC'), feature_group_count=C) + b
        mean = jnp.mean(y, axis=(1, 2), keepdims=True)
        var = jnp.var(y, axis=(1, 2), keepdims=True)
        yn = (y - mean) * lax.rsqrt(var + EPS) * gamma + beta
        return jnp.where(yn > 0, yn, alpha * yn)

    def _L0_attn_ref(x, W_qkv, b_qkv, W_out, b_out):
        import math
        import jax, jax.numpy as jnp
        import numpy as np
        EPS_DIV = 1e-07
        EPS_NORM = 1e-12

        def _l2_normalize(x, axis):
            n = jnp.sqrt(jnp.sum(x * x, axis=axis, keepdims=True))
            return x / jnp.maximum(n, EPS_NORM)
        b, N, C = x.shape
        qkv = x @ W_qkv + b_qkv
        q, k, v = jnp.split(qkv, 3, axis=2)
        q = q - jnp.mean(q, axis=2, keepdims=True)
        k = k - jnp.mean(k, axis=2, keepdims=True)
        q2 = q * q
        k2 = k * k
        q2s = jnp.sum(q2, axis=2, keepdims=True)
        k2s = jnp.sum(k2, axis=2, keepdims=True)
        k2 = _l2_normalize(k2 / (k2s + EPS_DIV), axis=-2)
        q2 = _l2_normalize(q2 / (q2s + EPS_DIV), axis=-1)
        kv = jnp.einsum('bnc,bnd->bcd', k2, v)
        t2 = jnp.einsum('bnc,bcd->bnd', q2, kv) / math.sqrt(N)
        attn = v + t2
        return attn @ W_out + b_out

    def _L0_ffn_ref(features, router_w1, router_b1, router_w2, router_b2, expert_w1, expert_b1, expert_w2, expert_b2, expert_w3, expert_b3):
        import jax, jax.numpy as jnp
        import numpy as np
        E, D, H, TOP_K = (6, 64, 64, 2)
        ROUTER_H = D // 2
        rh = jax.nn.relu(features @ router_w1 + router_b1)
        expert_logits = jax.nn.softmax(rh @ router_w2 + router_b2, axis=-1)
        top_w, top_i = jax.lax.top_k(expert_logits, TOP_K)
        routing_weights = jax.nn.softmax(top_w, axis=-1)
        h1 = jax.nn.relu(jnp.einsum('bsd,edh->bseh', features, expert_w1) + expert_b1)
        h2 = jax.nn.relu(jnp.einsum('bseh,ehf->bsef', h1, expert_w2) + expert_b2)
        expert_out = jnp.einsum('bsef,efo->bseo', h2, expert_w3) + expert_b3
        sel = jnp.take_along_axis(expert_out, top_i[:, :, :, None], axis=2)
        combined = jnp.sum(sel * routing_weights[..., None], axis=2)
        return combined
    h = _L0_tok_ref(x, L0_tok_w, L0_tok_b, L0_tok_gamma, L0_tok_beta, L0_tok_alpha)
    h = h + _L0_attn_ref(_layernorm(h, axis=-1), L0_attn_W_qkv, L0_attn_b_qkv, L0_attn_W_out, L0_attn_b_out)
    h = h + _L0_ffn_ref(_layernorm(h, axis=-1), L0_ffn_router_w1, L0_ffn_router_b1, L0_ffn_router_w2, L0_ffn_router_b2, L0_ffn_expert_w1, L0_ffn_expert_b1, L0_ffn_expert_w2, L0_ffn_expert_b2, L0_ffn_expert_w3, L0_ffn_expert_b3)
    return h

_drawn_inputs = setup_inputs


def setup_inputs(seed=0):
    import zlib

    import numpy as np

    out = dict(_drawn_inputs(seed))
    spreads = {'L0_tok_gamma': (1.0, 0.2),
     'L0_tok_beta': (0.0, 0.1),
     'L0_ffn_router_b1': (0.0, 0.285),
     'L0_ffn_router_b2': (0.0, 0.1),
     'L0_ffn_expert_b1': (0.0, 0.8),
     'L0_ffn_expert_b2': (0.0, 0.375),
     'L0_ffn_expert_b3': (0.0, 0.1)}
    factors = {'L0_attn_b_out': 3.626}
    for name, (base, spread) in spreads.items():
        noise = np.random.default_rng([zlib.crc32(name.encode()), seed]).standard_normal(out[name].shape)
        drawn = base * np.exp(spread * noise) if base else spread * noise
        out[name] = jnp.asarray(drawn.astype(out[name].dtype))
    for name, factor in factors.items():
        out[name] = (out[name] * factor).astype(out[name].dtype)
    return out
```

```python
from contextlib import ExitStack

import concourse.bass as bass
from concourse import mybir

F32 = mybir.dt.float32
F16 = mybir.dt.float16
ALU = mybir.AluOpType
ACT = mybir.ActivationFunctionType
AX = mybir.AxisListType.X

EPS_BATCH = 1e-3
EPS_LAYER = 1e-5
EPS_DIV = 1e-7
EPS_NORM = 1e-12


class Chain:

    def __init__(self, sem, steps):
        self.sem = sem
        self.steps = {name: n + 1 for n, name in enumerate(steps.split())}

    def at(self, step, pair):
        return len(self.steps) * pair + self.steps[step]


class Count:

    def __init__(self, sem, per):
        self.sem, self.per = sem, per

    def at(self, n, pair):
        return self.per * pair + n


def audio_tower(nc, x, w, const, out, E, H, RH, TAPS):
    B, TIN, C = x.shape
    T = out.shape[1]
    PAIRS = B // 2
    P = 2 * C
    NT = 3
    TP = T // NT
    G = 2 * NT
    J = E // 2
    TE = TP + TP % 2
    NX = TIN // TP
    assert P == 128 and C == H and T == NT * TP and TIN == 2 * T and TAPS == 5 and B % 4 == 0

    Q0, K0, V0, E0, R0 = 0, P, P + C, P + 2 * C, P + 2 * C + E * H
    WCOLS = R0 + RH

    with ExitStack() as ctx:
        def sb(name, shape, dt=F32):
            return ctx.enter_context(nc.sbuf_tensor(name, shape, dt))

        def bank(name, dt=F32):
            return ctx.enter_context(nc.psum_tensor(name, [128, 512 if dt == F32 else 1024], dt))

        def sem(name):
            return ctx.enter_context(nc.semaphore(name))

        const_in = sb("const_in", [128, 3, 128])
        ident, centre, average = (const_in[:, i, :] for i in range(3))
        ident16 = sb("ident16", [128, 128], F16)
        pick_in = sb("pick_in", [2 * E, J, 128])
        pick = sb("pick", [2 * E, J, 128], F16)
        rank = sb("rank", [128, E])
        minus_half = sb("minus_half", [128, G])
        stack = sb("stack", [128, WCOLS])
        stack_hi = sb("stack_hi", [128, WCOLS], F16)
        stack_lo = sb("stack_lo", [128, WCOLS], F16)
        head = sb("head", [C, 3 * C + 1])
        wvT, wout, bv = head[:, 0:2 * C], head[:, 2 * C:3 * C], head[:, 3 * C:]
        row_mean = sb("row_mean", [128, 4])
        bqc = sb("bqc", [128, 1])
        kv_row = sb("kv_row", [1, 2, C])
        kv_lo = sb("kv_lo", [1, NT, 2 * C], F16)
        kv_bias = sb("kv_bias", [2, NT, 2 * C], F16)
        ones2 = sb("ones2", [2, TP], F16)
        w2 = sb("w2", [128, J, 128])
        w3 = sb("w3", [128, J, C])
        b3 = sb("b3", [2 * E, C])
        b3_hi = sb("b3_hi", [2 * E, C], F16)
        b3_lo = sb("b3_lo", [2 * E, C], F16)
        wr2 = sb("wr2", [RH + 1, E])
        cols = sb("cols", [128, TAPS + 6 + 2 * J + 1])
        conv_w = cols[:, 0:TAPS]
        conv_b, gamma, beta, alpha, b_out, bq = (cols[:, TAPS + i:TAPS + i + 1] for i in range(6))
        b1 = cols[:, TAPS + 6:TAPS + 6 + J]
        b2 = cols[:, TAPS + 6 + J:TAPS + 6 + 2 * J]
        br1 = cols[0:RH, TAPS + 6 + 2 * J:]

        x_in = sb("x_in", [TP, 2, NX, 2, C])
        xT = sb("xT", [128, TIN + 4])
        y = sb("y", [128, T])
        stats = sb("stats", [128, 6])
        bn = sb("bn", [128, 12])
        z = sb("z", [128, NT, TP])
        below = sb("below", [128, NT, TP])
        h = sb("h", [128, NT, TP])
        hb = sb("hb", [128, NT, TP])
        sq1 = sb("sq1", [TP, NT, 2, C])
        ln1 = sb("ln1", [TP, 3, G])
        t1 = sb("t1", [TP, G, C])
        hl1 = sb("hl1", [TP, G, 2, C], F16)
        l1 = sb("l1", [128, G, TP], F16)
        k_sq = sb("k_sq", [TP, G, C])
        ks = sb("ks", [TP, 3, G])
        kk = sb("kk", [TP, G, 2, C])
        v1 = sb("v1", [TP, G, C + 1])
        q2 = sb("q2", [128, G, TP])
        kn = sb("kn", [C, 3, 2])
        kvn = sb("kvn", [128, 2, C + 2])
        at = sb("at", [TP, 8, G])
        att = sb("att", [TP, G, C])
        att_v = sb("att_v", [TP, G, C])
        h2 = sb("h2", [TP, 2, G, C])
        st2 = sb("st2", [TP, G, 6])
        ln2 = sb("ln2", [TP, 8, G])
        t2 = sb("t2", [TP, G, C])
        hl2 = sb("hl2", [TP, G, 2, C], F16)
        l2 = sb("l2", [128, G, TP], F16)
        rh = sb("rh", [RH + 1, G, TP])
        rt = sb("rt", [TP, 8, G, E])
        rs = sb("rs", [TP, 10, G])
        gate = sb("gate", [TP, G, 2, E], F16)
        gateT = sb("gateT", [2 * E, G, TP], F16)
        e1 = sb("e1", [128, J, G, TP])
        e2 = sb("e2", [128, J, G, TP])
        e2g = sb("e2g", [128, J, G, TP])
        y_out = sb("y_out", [TP, 2, G, C])

        bx = bank("bx")
        bk = [bank(f"bk{b}") for b in range(2)]
        bt = bank("bt")
        bl = bank("bl", F16)
        bs = bank("bs")
        bh = [bank(f"bh{i}") for i in range(2)]

        s_w = sem("weights_in")
        s_b = sem("low_bias_moved")
        SET = Chain(sem("setup"), "vw vwc bq bqc mean scaled centred bias hilo all")
        s_set = SET.sem
        s_fill = sem("filled")
        carrier = sem("carrier")
        x_ready = [sem(f"x_ready{i}") for i in range(2)]
        stored = [sem(f"stored{i}") for i in range(2)]

        XT = Chain(sem("x_turned"), "turn0 copy0 turn1 copy1")
        BN = Chain(sem("front"), "tap0 tap1 tap2 tap3 tap4 stats aggr mean dev var_c var var_eps"
                   " rstd scale shift0 shift normed below prelu")
        HB = Count(sem("h_biased"), 1)
        L1 = Chain(sem("layer_norm_1"), "centred square sum var rstd norm high low turn copy")
        KP = Count(sem("kv_product"), 2)
        KE = Count(sem("kv_taken"), 4)
        KN = Chain(sem("k_normed"), "sum eps recip k2 k4 kv least rlen kvn0 kvn1")
        QC = Chain(sem("q_squared"), "q0 sq0 q1 sq1 q4")
        HT = Count(sem("h_turned"), 1)
        AT = Chain(sem("attention"), "t2 eps recip n1 n2 least rlen scale scaled plus_v h2")
        L2 = Chain(sem("layer_norm_2"), "stats dm sm m2 dm2 var var_eps rstd mean centred norm"
                   " high low turn copy")
        RP = Count(sem("router_product"), 2)
        RA = Count(sem("router_relu"), 2)
        RT = Chain(sem("routing"), "logits max shifted exp sum recip prob max1 is1 ranked1 first1"
                   " one1 rest max2 is2 ranked2 first2 one2 gap egap egap1 w1 w2 g1 g2 gates"
                   " high low turn copy")
        E1P, E1A = Count(sem("expert1_product"), 2 * J), Count(sem("expert1_relu"), 2 * J)
        E2P, E2A = Count(sem("expert2_product"), 2 * J), Count(sem("expert2_relu"), 2 * J)
        GP, GA = Count(sem("gates_spread"), 2 * J), Count(sem("gated"), 2 * J)
        EO = Chain(sem("experts_out"), "product sum")

        def wait(eng, what, value):
            if not isinstance(value, int) or value > 0:
                eng.wait_ge(what.sem, value)

        weight_loads = [
            (const_in[:, :, :], const["squares"]), (cols[:, :], w["cols"]),
            (stack[:, :], w["stack"]), (head[:, :], w["head"]), (kv_row[:, 0, :], w["b_k"]),
            (pick_in[:, :, :], const["pick"]), (rank[:, :], const["rank"]),
            (b3[:, :], w["b3"]), (wr2[:, :], w["wr2"]), (w3[:, :, :], w["w3"]),
            (w2[:, :, :], w["w2"]),
        ]

        block = ctx.enter_context(nc.Block())

        def loaded(pair, slot):
            return 16 * (pair - slot) + 32

        def steps(eng, run):
            run(0, 0, True, False, False)
            run(1, 1, True, True, False)
            run(2, 0, True, True, True)
            run(3, 1, True, True, True)
            with eng.Fori(2, PAIRS // 2) as half:
                for parity in range(2):
                    run(2 * half + parity, parity, True, True, True)
            run(PAIRS, 0, False, True, True)
            run(PAIRS + 1, 1, False, False, True)

        @block.sync
        def _(sp):
            def load(pair, slot):
                for b in range(2):
                    sp.dma_start(x_in[:, slot, :, b, :],
                                 x[bass.ds(2 * pair + b, 1)].rearrange("o (p j) c -> p (o j) c", j=NX)
                                 ).then_inc(x_ready[slot], 16)

            load(0, 0)
            load(1, 1)
            for dst, src in weight_loads[0::2]:
                sp.dma_start(dst, src).then_inc(s_w, 16)

            def ahead(pair, slot):
                wait(sp, XT, XT.at("turn1", pair - 2))
                load(pair, slot)

            ahead(2, 0)
            ahead(3, 1)
            with sp.Fori(2, PAIRS // 2) as half:
                for parity in range(2):
                    ahead(2 * half + parity, parity)

        @block.gpsimd
        def _(pool):
            pool.wait_ge(SET.sem, SET.at("hilo", 0))
            pool.dma_start(kv_bias[1:2, :, :], kv_lo[:, :, :]).then_inc(s_b, 16)
            pool.wait_ge(SET.sem, SET.at("all", 0))

            def step(s, slot, F, A, M):
                f, a, m = s, s - 1, s - 2
                if A:
                    wait(pool, KN, KN.at("k2", a))
                    nc.gpsimd.tensor_tensor(kk[:, :, 1, :], kk[:, :, 0, :], kk[:, :, 0, :],
                                            ALU.mult).then_inc(KN.sem, 1)
                    wait(pool, KN, KN.at("k4", a))
                    wait(pool, QC, QC.at("sq1", a))
                    nc.gpsimd.tensor_tensor(q2[C:2 * C, :, :], q2[C:2 * C, :, :], q2[C:2 * C, :, :],
                                            ALU.mult).then_inc(QC.sem, 1)
                if F:
                    wait(pool, BN, BN.at("var_eps", f))
                    if A:
                        wait(pool, QC, QC.at("q4", a))
                    nc.gpsimd.tensor_tensor(bn[:, 5:6], bn[:, 4:5], minus_half[:, 0:1],
                                            ALU.pow).then_inc(BN.sem, 1)
                if A:
                    wait(pool, KN, KN.at("least", a))
                    wait(pool, QC, QC.at("q4", a))
                    if F:
                        wait(pool, BN, BN.at("rstd", f))
                    nc.gpsimd.tensor_tensor(kn[:, 1, :], kn[:, 0, :], minus_half[0:C, 0:2],
                                            ALU.pow).then_inc(KN.sem, 1)
                if F:
                    wait(pool, BN, BN.at("prelu", f))
                    if A:
                        wait(pool, KN, KN.at("rlen", a))
                    wait(pool, HT, HT.at(1, f - 1))
                    pool.sem_inc(carrier)
                    nc.gpsimd.tensor_scalar(hb[:, :, :], h[:, :, :], b_out, None,
                                            ALU.add).then_inc(HB.sem, 1)
                if A:
                    wait(pool, AT, AT.at("least", a))
                    nc.gpsimd.tensor_tensor(at[:, 5, :], at[:, 4, :], minus_half[0:TP, :],
                                            ALU.pow).then_inc(AT.sem, 1)
                    wait(pool, AT, AT.at("scaled", a))
                    wait(pool, KE, KE.at(4, a))
                    nc.gpsimd.tensor_tensor(att_v[:, :, :], att[:, :, :], v1[:, :, 0:C],
                                            ALU.add).then_inc(AT.sem, 1)
                if F:
                    wait(pool, L1, L1.at("var", f))
                    nc.gpsimd.tensor_tensor(ln1[:, 2, :], ln1[:, 1, :], minus_half[0:TP, :],
                                            ALU.pow).then_inc(L1.sem, 1)
                if A:
                    wait(pool, L2, L2.at("var_eps", a))
                    nc.gpsimd.tensor_tensor(ln2[:, 6, :], ln2[:, 5, :], minus_half[0:TP, :],
                                            ALU.pow).then_inc(L2.sem, 1)
                if F:
                    wait(pool, L1, L1.at("high", f))
                    nc.gpsimd.tensor_tensor(hl1[:, :, 1, :], t1[:, :, :], hl1[:, :, 0, :],
                                            ALU.subtract).then_inc(L1.sem, 1)
                if A:
                    wait(pool, L2, L2.at("high", a))
                    nc.gpsimd.tensor_tensor(hl2[:, :, 1, :], t2[:, :, :], hl2[:, :, 0, :],
                                            ALU.subtract).then_inc(L2.sem, 1)

            steps(pool, step)

        @block.tensor
        def _(pe):
            n_w = 16 * len(weight_loads)
            pe.wait_ge(s_w, n_w)
            nc.tensor.matmul(bs[:, 0:C], wvT, wout, start=True, stop=True)
            nc.tensor.matmul(bx[0:1, 0:C], bv, wout, start=True, stop=True
                             ).then_inc(s_set, 1)
            pe.wait_ge(s_set, SET.at("vwc", 0))
            nc.tensor.matmul(bs[:, 0:1], centre, bq, start=True, stop=True
                             ).then_inc(s_set, 1)
            pe.wait_ge(s_set, SET.at("all", 0))
            pe.wait_ge(s_b, 16)
            pe.wait_ge(s_fill, 8)

            def turn_split(bank_, hl, chain):
                for g in range(G):
                    i = nc.tensor.transpose(bank_[:, g * TE:g * TE + TP],
                                            hl[:, g, :, :].rearrange("p a c -> p (a c)"),
                                            ident16[0:TP, 0:TP])
                i.then_inc(chain.sem, 1)

            def split_product(dst, l, col, n, b):
                rhs = l[:, b * NT:(b + 1) * NT, :]
                nc.tensor.matmul(dst, stack_hi[:, col:col + n], rhs, start=True, stop=False)
                return nc.tensor.matmul(dst, stack_lo[:, col:col + n], rhs, start=False, stop=True)

            def expert1(m, n):
                j, b = n // 2, n % 2
                if n == 0:
                    wait(pe, L2, L2.at("copy", m))
                if n < 2:
                    wait(pe, E2A, E2A.at(2 * J - 1 + n, m - 1))
                else:
                    wait(pe, E1A, E1A.at(n - 1, m))
                split_product(bh[n % 2][:, 0:T], l2, E0 + j * 128, 128, b).then_inc(E1P.sem, 1)

            def expert2(m, n):
                j, b = n // 2, n % 2
                wait(pe, E1A, E1A.at(2 * J if n < 2 else n + 1, m))
                if n >= 2:
                    wait(pe, E2A, E2A.at(n - 1, m))
                nc.tensor.matmul(bh[n % 2][:, 0:T], w2[:, j, :], e1[:, j, b * NT:(b + 1) * NT, :],
                                 start=True, stop=True).then_inc(E2P.sem, 1)

            def spread(m, A, n):
                j, b = n // 2, n % 2
                if n == 0:
                    wait(pe, RT, RT.at("copy", m))
                if n < 2:
                    if A:
                        wait(pe, KE, KE.at(2 * n + 2, m + 1))
                    else:
                        wait(pe, RA, RA.at(n + 1, m))
                else:
                    wait(pe, GA, GA.at(n - 1, m))
                nc.tensor.matmul(bk[n % 2][:, 0:T], pick[:, j, :], gateT[:, b * NT:(b + 1) * NT, :],
                                 start=True, stop=True).then_inc(GP.sem, 1)

            def step(s, slot, F, A, M):
                f, a, m = s, s - 1, s - 2
                if F:
                    pe.wait_ge(x_ready[slot], loaded(s, slot))
                    for half in range(2):
                        if half == 0:
                            wait(pe, AT, AT.at("h2", f - 2))
                        else:
                            wait(pe, XT, XT.at("copy0", f))
                        for j in range(NX // 2):
                            i = nc.tensor.transpose(
                                bx[:, j * TP:(j + 1) * TP],
                                x_in[:, slot, half * NX // 2 + j, :, :].rearrange("p b c -> p (b c)"),
                                ident[0:TP, 0:TP])
                        i.then_inc(XT.sem, 1)
                if M:
                    wait(pe, L2, L2.at("low", m))
                    wait(pe, RT, RT.at("copy", m - 1))
                    turn_split(bl, hl2, L2)
                if A:
                    wait(pe, L1, L1.at("low", a))
                    if M:
                        wait(pe, L2, L2.at("copy", m))
                    turn_split(bl, hl1, L1)
                if M:
                    wait(pe, L2, L2.at("copy", m))
                    for b in range(2):
                        wait(pe, GA, GA.at(2 * J - 1 + b, m - 1))
                        split_product(bk[b][0:RH, 0:T], l2, R0, RH, b).then_inc(RP.sem, 1)
                    for n in range(0, J):
                        expert1(m, n)
                if A:
                    wait(pe, L1, L1.at("copy", a))
                    for b in range(2):
                        if M:
                            wait(pe, RA, RA.at(b + 1, m))
                        wait(pe, KE, KE.at(2 * b + 2, a - 1))
                        nc.tensor.matmul(bk[b][0:TP, 0:NT * 2 * C], ones2[:, :], kv_bias[:, :, :],
                                         start=True, stop=False, skip_group_check=True)
                        for j in range(NT):
                            dst = bk[b][0:TP, j * 2 * C:(j + 1) * 2 * C]
                            nc.tensor.matmul(dst, l1[:, b * NT + j, :], stack_hi[:, K0:E0],
                                             start=False, stop=False, skip_group_check=True)
                            i = nc.tensor.matmul(dst, l1[:, b * NT + j, :], stack_lo[:, K0:E0],
                                                 start=False, stop=j == NT - 1, skip_group_check=True)
                        i.then_inc(KP.sem, 1)
                if M:
                    wait(pe, RA, RA.at(2, m))
                    wait(pe, KN, KN.at("kvn1", m))
                    for g in range(G):
                        i = nc.tensor.matmul(bs[0:TP, g * E:(g + 1) * E], rh[:, g, :], wr2[:, :],
                                             start=True, stop=True)
                    i.then_inc(RT.sem, 1)
                    for n in range(J, 2 * J):
                        expert1(m, n)
                if A:
                    for b in range(2):
                        if b == 0:
                            if F:
                                wait(pe, XT, XT.at("copy1", f))
                            else:
                                wait(pe, AT, AT.at("h2", a - 1))
                        else:
                            wait(pe, QC, QC.at("sq0", a))
                        split_product(bx[:, 0:T], l1, Q0, 128, b).then_inc(QC.sem, 1)
                if F:
                    wait(pe, BN, BN.at("aggr", f))
                    if M:
                        wait(pe, RT, RT.at("shifted", m))
                    wait(pe, KN, KN.at("kvn1", f - 2))
                    nc.tensor.matmul(bs[:, 0:1], average, bn[:, 0:1], start=True, stop=True
                                     ).then_inc(BN.sem, 1)
                if M:
                    for n in range(0, 2):
                        expert2(m, n)
                if F:
                    wait(pe, BN, BN.at("var_c", f))
                    nc.tensor.matmul(bs[:, 1:2], average, bn[:, 3:4], start=True, stop=True
                                     ).then_inc(BN.sem, 1)
                if M:
                    for n in range(2, 4):
                        expert2(m, n)
                if A:
                    wait(pe, KN, KN.at("k4", a))
                    wait(pe, KE, KE.at(4, a))
                    if M:
                        wait(pe, RT, RT.at("shifted", m))
                    if F:
                        wait(pe, BN, BN.at("shift0", f))
                    for b in range(2):
                        for j in range(NT):
                            g = b * NT + j
                            i = nc.tensor.matmul(bs[:, b * (C + 1):(b + 1) * (C + 1)],
                                                 kk[:, g, :, :], v1[:, g, :],
                                                 start=j == 0, stop=j == NT - 1)
                    i.then_inc(KN.sem, 1)
                if M:
                    for n in range(4, 6):
                        expert2(m, n)
                    wait(pe, RT, RT.at("low", m))
                    if A:
                        wait(pe, L1, L1.at("copy", a))
                    for g in range(G):
                        i = nc.tensor.transpose(bl[0:2 * E, g * TE:g * TE + TP],
                                                gate[:, g, :, :].rearrange("p a e -> p (a e)"),
                                                ident16[0:TP, 0:TP])
                    i.then_inc(RT.sem, 1)
                    for n in range(0, 2):
                        spread(m, A, n)
                if A:
                    wait(pe, HB, HB.at(1, a))
                    wait(pe, QC, QC.at("sq1", a))
                    for j in range(NT):
                        i = nc.tensor.transpose(bx[0:TP, j * 128:(j + 1) * 128], hb[:, j, :],
                                                ident)
                    i.then_inc(HT.sem, 1)
                    wait(pe, QC, QC.at("q4", a))
                    wait(pe, KN, KN.at("kvn1", a))
                    wait(pe, EO, EO.at("sum", a - 2))
                    for g in range(G):
                        i = nc.tensor.matmul(bt[0:TP, g * (C + 2):(g + 1) * (C + 2)], q2[:, g, :],
                                             kvn[:, g // NT, :], start=True, stop=True)
                    i.then_inc(AT.sem, 1)
                if M:
                    for n in range(2, 4):
                        spread(m, A, n)
                if F:
                    wait(pe, BN, BN.at("prelu", f))
                    if A:
                        wait(pe, AT, AT.at("scaled", a))
                    for j in range(NT):
                        i = nc.tensor.matmul(bt[0:TP, j * 128:(j + 1) * 128], h[:, j, :],
                                             centre, start=True, stop=True)
                    i.then_inc(L1.sem, 1)
                if M:
                    for n in range(4, 6):
                        spread(m, A, n)
                    wait(pe, GA, GA.at(2 * J, m))
                    if F:
                        wait(pe, L1, L1.at("norm", f))
                    elif A:
                        wait(pe, AT, AT.at("scaled", a))
                    else:
                        wait(pe, EO, EO.at("sum", m - 1))
                    for g in range(G):
                        dst = bt[0:TP, g * C:(g + 1) * C]
                        nc.tensor.matmul(dst, gateT[:, g, :], b3_hi[:, :], start=True, stop=False)
                        nc.tensor.matmul(dst, gateT[:, g, :], b3_lo[:, :], start=False, stop=False)
                        for j in range(J):
                            i = nc.tensor.matmul(dst, e2g[:, j, g, :], w3[:, j, :],
                                                 start=False, stop=j == J - 1)
                    i.then_inc(EO.sem, 1)

            steps(pe, step)

        @block.scalar
        def _(act):
            for dst, src in weight_loads[1::2]:
                act.dma_start(dst, src).then_inc(s_w, 16)
            act.wait_ge(s_set, SET.at("all", 0))
            act.wait_ge(s_fill, 8)

            def expert_relu(P_, A_, dst, bias, m, n):
                j, b = n // 2, n % 2
                wait(act, P_, P_.at(n + 1, m))
                nc.scalar.activation(dst[:, j, b * NT:(b + 1) * NT, :],
                                     bh[n % 2][:, 0:T].rearrange("p (j t) -> p j t", j=NT),
                                     ACT.Relu, bias=bias[:, j:j + 1]).then_inc(A_.sem, 1)

            def relu1(m, n):
                if n == 0:
                    wait(act, E2P, E2P.at(2 * J, m - 1))
                expert_relu(E1P, E1A, e1, b1, m, n)

            def relu2(m, n):
                if n == 0:
                    wait(act, GA, GA.at(2 * J, m - 1))
                expert_relu(E2P, E2A, e2, b2, m, n)

            def step(s, slot, F, A, M):
                f, a, m = s, s - 1, s - 2
                if F:
                    for half in range(2):
                        wait(act, XT, XT.at(f"turn{half}", f))
                        if half == 0:
                            wait(act, BN, BN.at("tap4", f - 1))
                        dst = xT[:, 1:1 + TIN].rearrange("p (t j) -> p j t", j=NX)
                        nc.scalar.activation(dst[:, half * NX // 2:(half + 1) * NX // 2, :],
                                             bx[:, 0:T].rearrange("p (j t) -> p j t", j=NX // 2),
                                             ACT.Copy).then_inc(XT.sem, 1)
                    wait(act, XT, XT.at("copy1", f))
                    wait(act, BN, BN.at("prelu", f - 1))
                    nc.scalar.activation(y[:, :], xT[:, 0:2 * T:2], ACT.Identity, bias=conv_b,
                                         scale=conv_w[:, 0:1]).then_inc(BN.sem, 1)
                if M:
                    for b in range(2):
                        wait(act, RP, RP.at(b + 1, m))
                        if b == 0:
                            wait(act, RT, RT.at("logits", m - 1))
                        nc.scalar.activation(rh[0:RH, b * NT:(b + 1) * NT, :],
                                             bk[b][0:RH, 0:T].rearrange("p (j t) -> p j t", j=NT),
                                             ACT.Relu, bias=br1).then_inc(RA.sem, 1)
                    for n in range(0, J):
                        relu1(m, n)
                if A:
                    for b in range(2):
                        kv = bk[b][0:TP, 0:NT * 2 * C].rearrange("p (j c) -> p j c", j=NT)
                        wait(act, KP, KP.at(b + 1, a))
                        if b == 0:
                            wait(act, KN, KN.at("kv", a - 1))
                            wait(act, AT, AT.at("plus_v", a - 1))
                        nc.scalar.activation(k_sq[:, b * NT:(b + 1) * NT, :], kv[:, :, 0:C],
                                             ACT.Square).then_inc(KE.sem, 1)
                        nc.scalar.activation(v1[:, b * NT:(b + 1) * NT, 0:C], kv[:, :, C:2 * C],
                                             ACT.Copy).then_inc(KE.sem, 1)
                if M:
                    wait(act, RT, RT.at("shifted", m))
                    nc.scalar.activation(rt[:, 1, :, :], rt[:, 0, :, :], ACT.Exp).then_inc(RT.sem, 1)
                    for n in range(J, 2 * J):
                        relu1(m, n)
                if A:
                    for b in range(2):
                        wait(act, QC, QC.at(f"q{b}", a))
                        if b == 0:
                            wait(act, AT, AT.at("t2", a - 1))
                        nc.scalar.activation(q2[:, b * NT:(b + 1) * NT, :],
                                             bx[:, 0:T].rearrange("p (j t) -> p j t", j=NT),
                                             ACT.Square, bias=bqc[:, :]).then_inc(QC.sem, 1)
                if M:
                    for n in range(0, 2):
                        relu2(m, n)
                    wait(act, RT, RT.at("gap", m))
                    nc.scalar.activation(rs[:, 6, :], rs[:, 5, :], ACT.Exp).then_inc(RT.sem, 1)
                    for n in range(2, 4):
                        relu2(m, n)
                if F:
                    wait(act, BN, BN.at("shift", f))
                    nc.scalar.activation(z[:, :, :], y[:, :].rearrange("p (t j) -> p j t", j=NT),
                                         ACT.Identity, bias=bn[:, 8:9], scale=bn[:, 6:7]
                                         ).then_inc(BN.sem, 1)
                if M:
                    for n in range(4, 6):
                        relu2(m, n)
                if F:
                    wait(act, L1, L1.at("centred", f))
                    nc.scalar.activation(sq1[:, :, :, :].rearrange("p j b c -> p (j b c)"),
                                         bt[0:TP, 0:NT * 128], ACT.Square).then_inc(L1.sem, 1)
                if M:
                    wait(act, EO, EO.at("sum", m))
                    for b in range(2):
                        act.dma_start(out[bass.ds(2 * m + b, 1)].rearrange("o (p j) c -> p (o j) c", j=NT),
                                      y_out[:, slot, b * NT:(b + 1) * NT, :]
                                      ).then_inc(stored[slot], 16)

            steps(act, step)
            for slot in range(2):
                act.wait_ge(stored[slot], 16 * PAIRS)

        @block.vector
        def _(dve):
            V = nc.vector
            V.memset(minus_half[:, :], -0.5).then_inc(s_fill, 1)
            V.memset(xT[:, :], 0.0).then_inc(s_fill, 1)
            V.memset(v1[:, :, :], 1.0).then_inc(s_fill, 1)
            V.memset(kvn[:, :, :], 0.0).then_inc(s_fill, 1)
            V.memset(rh[RH:RH + 1, :, :], 1.0).then_inc(s_fill, 1)
            V.memset(ones2[:, :], 1.0).then_inc(s_fill, 1)
            dve.wait_ge(s_fill, 6)
            V.memset(kvn[0:C, :, C:C + 1], 1.0).then_inc(s_fill, 1)
            V.memset(kvn[C:2 * C, :, C + 1:C + 2], 1.0).then_inc(s_fill, 1)
            dve.wait_ge(s_w, 16 * len(weight_loads))
            V.tensor_copy(ident16[:, :], ident)
            V.tensor_copy(pick[:, :, :], pick_in[:, :, :])
            V.tensor_copy(b3_hi[:, :], b3[:, :]).then_inc(s_fill, 1)
            dve.wait_ge(s_set, SET.at("vw", 0))
            V.tensor_copy(stack[:, V0:V0 + C], bs[:, 0:C])
            V.tensor_copy(kv_row[:, 1, :], bx[0:1, 0:C]).then_inc(s_set, 1)
            dve.wait_ge(s_set, SET.at("bq", 0))
            V.tensor_copy(bqc[:, :], bs[:, 0:1]).then_inc(s_set, 1)
            V.tensor_reduce(row_mean[:, 0:1], stack[:, Q0:Q0 + C], AX, ALU.add, negate=True)
            V.tensor_reduce(row_mean[:, 1:2], stack[:, K0:K0 + C], AX, ALU.add, negate=True)
            V.tensor_reduce(row_mean[0:1, 2:3], kv_row[:, 0, :], AX, ALU.add, negate=True
                            ).then_inc(s_set, 1)
            dve.wait_ge(s_set, SET.at("mean", 0))
            V.tensor_scalar(row_mean[:, 0:2], row_mean[:, 0:2], 1.0 / C, None, ALU.mult)
            V.tensor_scalar(row_mean[0:1, 2:3], row_mean[0:1, 2:3], 1.0 / C, None, ALU.mult
                            ).then_inc(s_set, 1)
            dve.wait_ge(s_set, SET.at("scaled", 0))
            V.tensor_scalar(stack[:, Q0 + C:Q0 + 2 * C], stack[:, Q0:Q0 + C], row_mean[:, 0:1], None,
                            ALU.add)
            V.tensor_scalar(stack[:, K0:K0 + C], stack[:, K0:K0 + C], row_mean[:, 1:2], None, ALU.add)
            V.tensor_scalar(kv_row[:, 0, :], kv_row[:, 0, :], row_mean[0:1, 2:3], None, ALU.add
                            ).then_inc(s_set, 1)
            dve.wait_ge(s_set, SET.at("centred", 0))
            V.tensor_copy(stack[:, Q0:Q0 + C], stack[:, Q0 + C:Q0 + 2 * C])
            for j in range(NT):
                i = V.tensor_copy(kv_bias[0:1, j, :], kv_row[:, :, :].rearrange("p a c -> p (a c)"))
            i.then_inc(s_set, 1)
            dve.wait_ge(s_set, SET.at("bias", 0))
            V.tensor_copy(stack_hi[:, :], stack[:, :])
            for j in range(NT):
                i = V.tensor_tensor(kv_lo[:, j, :], kv_row[:, :, :].rearrange("p a c -> p (a c)"),
                                    kv_bias[0:1, j, :], ALU.subtract)
            i.then_inc(s_set, 1)
            dve.wait_ge(s_set, SET.at("hilo", 0))
            V.tensor_tensor(b3_lo[:, :], b3[:, :], b3_hi[:, :], ALU.subtract)
            V.tensor_tensor(stack_lo[:, :], stack[:, :], stack_hi[:, :], ALU.subtract
                            ).then_inc(s_set, 1)
            dve.wait_ge(s_fill, 9)

            def per_token(col, n=C):
                return col.unsqueeze(2).to_broadcast([TP, G, n])

            def split_copy(l, bank_, chain, pair):
                wait(dve, chain, chain.at("turn", pair))
                V.tensor_copy(l[:, :, :], bank_[:, 0:G * TE].rearrange("p (g t) -> p g t", g=G)[:, :, 0:TP]
                              ).then_inc(chain.sem, 1)

            def route_pick(src, k, names, m):
                top, isit, ranked, first, one = names
                most = rs[:, 2 + 5 * k, :]
                V.tensor_reduce(most, rt[:, src, :, :], AX, ALU.max).then_inc(RT.sem, 1)
                wait(dve, RT, RT.at(top, m))
                V.tensor_tensor(rt[:, 3, :, :], rt[:, src, :, :], per_token(most, E),
                                ALU.is_equal).then_inc(RT.sem, 1)
                wait(dve, RT, RT.at(isit, m))
                V.tensor_tensor(rt[:, 3, :, :], rt[:, 3, :, :],
                                rank[0:TP, :].unsqueeze(1).to_broadcast([TP, G, E]),
                                ALU.mult).then_inc(RT.sem, 1)
                wait(dve, RT, RT.at(ranked, m))
                V.tensor_reduce(rs[:, 3, :], rt[:, 3, :, :], AX, ALU.max).then_inc(RT.sem, 1)
                wait(dve, RT, RT.at(first, m))
                V.tensor_tensor(rt[:, 4 + k, :, :], rt[:, 3, :, :], per_token(rs[:, 3, :], E),
                                ALU.is_equal).then_inc(RT.sem, 1)
                wait(dve, RT, RT.at(one, m))

            def gated(m, n):
                j, b = n // 2, n % 2
                wait(dve, E2A, E2A.at(n + 1, m))
                wait(dve, GP, GP.at(n + 1, m))
                if n == 0:
                    wait(dve, EO, EO.at("product", m - 1))
                V.tensor_tensor(e2g[:, j, b * NT:(b + 1) * NT, :], e2[:, j, b * NT:(b + 1) * NT, :],
                                bk[n % 2][:, 0:T].rearrange("p (j t) -> p j t", j=NT),
                                ALU.mult).then_inc(GA.sem, 1)

            def step(s, slot, F, A, M):
                f, a, m = s, s - 1, s - 2
                if M:
                    wait(dve, E1P, E1P.at(2 * J, m - 1))
                    split_copy(l2, bl, L2, m)
                if A:
                    wait(dve, QC, QC.at("q1", a - 1))
                    split_copy(l1, bl, L1, a)
                if F:
                    for k in range(1, TAPS):
                        wait(dve, BN, BN.at(f"tap{k - 1}", f))
                        V.scalar_tensor_tensor(out=y[:, :], in0=xT[:, k:k + 2 * T:2],
                                               scalar=conv_w[:, k:k + 1], in1=y[:, :],
                                               op0=ALU.mult, op1=ALU.add).then_inc(BN.sem, 1)
                    wait(dve, BN, BN.at("tap4", f))
                    V.bn_stats(stats[:, :], y[:, :]).then_inc(BN.sem, 1)
                    wait(dve, BN, BN.at("stats", f))
                    dve.sem_inc(carrier)
                    V.bn_aggr(bn[:, 0:2], stats[:, :]).then_inc(BN.sem, 1)
                if M:
                    lg = bs[0:TP, 0:G * E].rearrange("p (g e) -> p g e", e=E)
                    wait(dve, RT, RT.at("logits", m))
                    V.tensor_reduce(rs[:, 0, :], lg, AX, ALU.max).then_inc(RT.sem, 1)
                    wait(dve, RT, RT.at("max", m))
                    V.tensor_tensor(rt[:, 0, :, :], lg, per_token(rs[:, 0, :], E),
                                    ALU.subtract).then_inc(RT.sem, 1)
                if A:
                    wait(dve, KE, KE.at(3, a))
                    V.tensor_reduce(ks[:, 0, :], k_sq[:, :, :], AX, ALU.add).then_inc(KN.sem, 1)
                    wait(dve, KN, KN.at("sum", a))
                    V.tensor_scalar(ks[:, 1, :], ks[:, 0, :], EPS_DIV, None, ALU.add
                                    ).then_inc(KN.sem, 1)
                    wait(dve, KN, KN.at("eps", a))
                    V.reciprocal(ks[:, 2, :], ks[:, 1, :]).then_inc(KN.sem, 1)
                    wait(dve, KN, KN.at("recip", a))
                    V.tensor_tensor(kk[:, :, 0, :], k_sq[:, :, :], per_token(ks[:, 2, :]),
                                    ALU.mult).then_inc(KN.sem, 1)
                if F:
                    wait(dve, BN, BN.at("mean", f))
                    V.tensor_tensor(bn[:, 2:3], bn[:, 0:1], bs[:, 0:1], ALU.subtract
                                    ).then_inc(BN.sem, 1)
                    wait(dve, BN, BN.at("dev", f))
                    V.scalar_tensor_tensor(out=bn[:, 3:4], in0=bn[:, 2:3], scalar=bn[:, 2:3],
                                           in1=bn[:, 1:2], op0=ALU.mult, op1=ALU.add
                                           ).then_inc(BN.sem, 1)
                if M:
                    wait(dve, RT, RT.at("exp", m))
                    V.tensor_reduce(rs[:, 1, :], rt[:, 1, :, :], AX, ALU.add).then_inc(RT.sem, 1)
                    wait(dve, RT, RT.at("sum", m))
                    V.reciprocal(rs[:, 4, :], rs[:, 1, :]).then_inc(RT.sem, 1)
                    wait(dve, RT, RT.at("recip", m))
                    V.tensor_tensor(rt[:, 2, :, :], rt[:, 1, :, :], per_token(rs[:, 4, :], E),
                                    ALU.mult).then_inc(RT.sem, 1)
                    wait(dve, RT, RT.at("prob", m))
                    route_pick(2, 0, ("max1", "is1", "ranked1", "first1", "one1"), m)
                    V.scalar_tensor_tensor(out=rt[:, 6, :, :], in0=rt[:, 4, :, :], scalar=-2.0,
                                           in1=rt[:, 2, :, :], op0=ALU.mult, op1=ALU.add
                                           ).then_inc(RT.sem, 1)
                    wait(dve, RT, RT.at("rest", m))
                if F:
                    wait(dve, BN, BN.at("var", f))
                    V.tensor_scalar(bn[:, 4:5], bs[:, 1:2], EPS_BATCH, None, ALU.add
                                    ).then_inc(BN.sem, 1)
                if M:
                    route_pick(6, 1, ("max2", "is2", "ranked2", "first2", "one2"), m)
                    V.tensor_tensor(rs[:, 5, :], rs[:, 7, :], rs[:, 2, :], ALU.subtract
                                    ).then_inc(RT.sem, 1)
                if F:
                    wait(dve, BN, BN.at("rstd", f))
                    V.tensor_tensor(bn[:, 6:7], bn[:, 5:6], gamma, ALU.mult).then_inc(BN.sem, 1)
                    wait(dve, BN, BN.at("scale", f))
                    V.tensor_tensor(bn[:, 7:8], bn[:, 6:7], bs[:, 0:1], ALU.mult
                                    ).then_inc(BN.sem, 1)
                    wait(dve, BN, BN.at("shift0", f))
                    V.tensor_tensor(bn[:, 8:9], beta, bn[:, 7:8], ALU.subtract
                                    ).then_inc(BN.sem, 1)
                if A:
                    wait(dve, KN, KN.at("kv", a))
                    kv = bs[:, 0:2 * (C + 1)].rearrange("p (b c) -> p b c", b=2)
                    V.tensor_scalar(kn[:, 0, :], kv[C:2 * C, :, C], EPS_NORM ** 2, None, ALU.max
                                    ).then_inc(KN.sem, 1)
                    wait(dve, KN, KN.at("rlen", a))
                    wait(dve, AT, AT.at("t2", a - 1))
                    for b in range(2):
                        V.tensor_scalar(kvn[0:C, b, 0:C], kv[0:C, b, 0:C], kn[:, 1, b:b + 1],
                                        float(T) ** -0.5, ALU.mult, ALU.mult).then_inc(KN.sem, 1)
                if M:
                    wait(dve, RT, RT.at("egap", m))
                    V.tensor_scalar(rs[:, 8, :], rs[:, 6, :], 1.0, None, ALU.add).then_inc(RT.sem, 1)
                    wait(dve, RT, RT.at("egap1", m))
                    V.reciprocal(rs[:, 9, :], rs[:, 8, :]).then_inc(RT.sem, 1)
                    wait(dve, RT, RT.at("w1", m))
                    V.tensor_tensor(rs[:, 8, :], rs[:, 9, :], rs[:, 6, :], ALU.mult
                                    ).then_inc(RT.sem, 1)
                    wait(dve, RT, RT.at("w2", m))
                    V.tensor_tensor(rt[:, 4, :, :], rt[:, 4, :, :], per_token(rs[:, 9, :], E),
                                    ALU.mult).then_inc(RT.sem, 1)
                    V.tensor_tensor(rt[:, 5, :, :], rt[:, 5, :, :], per_token(rs[:, 8, :], E),
                                    ALU.mult).then_inc(RT.sem, 1)
                    wait(dve, RT, RT.at("g2", m))
                    V.tensor_tensor(rt[:, 7, :, :], rt[:, 4, :, :], rt[:, 5, :, :], ALU.add
                                    ).then_inc(RT.sem, 1)
                    wait(dve, RT, RT.at("gates", m))
                    V.tensor_copy(gate[:, :, 0, :], rt[:, 7, :, :]).then_inc(RT.sem, 1)
                    wait(dve, RT, RT.at("high", m))
                    V.tensor_tensor(gate[:, :, 1, :], rt[:, 7, :, :], gate[:, :, 0, :],
                                    ALU.subtract).then_inc(RT.sem, 1)
                    wait(dve, EO, EO.at("product", m - 1))
                    wait(dve, RT, RT.at("turn", m))
                    V.tensor_copy(gateT[:, :, :], bl[0:2 * E, 0:G * TE].rearrange(
                        "p (g t) -> p g t", g=G)[:, :, 0:TP]).then_inc(RT.sem, 1)
                if F:
                    wait(dve, BN, BN.at("normed", f))
                    V.tensor_scalar(below[:, :, :], z[:, :, :], 0.0, alpha, ALU.min, ALU.mult
                                    ).then_inc(BN.sem, 1)
                    wait(dve, L1, L1.at("centred", f - 1))
                    wait(dve, HB, HB.at(1, f - 1))
                    wait(dve, BN, BN.at("below", f))
                    V.scalar_tensor_tensor(out=h[:, :, :], in0=z[:, :, :], scalar=0.0,
                                           in1=below[:, :, :], op0=ALU.max, op1=ALU.add
                                           ).then_inc(BN.sem, 1)
                if A:
                    t2p = bt[0:TP, 0:G * (C + 2)].rearrange("p (g c) -> p g c", g=G)
                    wait(dve, AT, AT.at("t2", a))
                    V.tensor_scalar(at[:, 0, :], t2p[:, :, C], EPS_DIV, None, ALU.add
                                    ).then_inc(AT.sem, 1)
                    wait(dve, AT, AT.at("eps", a))
                    V.reciprocal(at[:, 1, :], at[:, 0, :]).then_inc(AT.sem, 1)
                    wait(dve, AT, AT.at("recip", a))
                    V.tensor_tensor(at[:, 2, :], t2p[:, :, C + 1], at[:, 1, :], ALU.mult
                                    ).then_inc(AT.sem, 1)
                    wait(dve, AT, AT.at("n1", a))
                    V.tensor_tensor(at[:, 3, :], at[:, 2, :], at[:, 1, :], ALU.mult
                                    ).then_inc(AT.sem, 1)
                    wait(dve, AT, AT.at("n2", a))
                    V.tensor_scalar(at[:, 4, :], at[:, 3, :], EPS_NORM ** 2, None, ALU.max
                                    ).then_inc(AT.sem, 1)
                if M:
                    for n in range(0, 2):
                        gated(m, n)
                if A:
                    wait(dve, AT, AT.at("rlen", a))
                    V.tensor_tensor(at[:, 6, :], at[:, 5, :], at[:, 1, :], ALU.mult
                                    ).then_inc(AT.sem, 1)
                    wait(dve, AT, AT.at("scale", a))
                    V.tensor_tensor(att[:, :, :], t2p[:, :, 0:C], per_token(at[:, 6, :]), ALU.mult
                                    ).then_inc(AT.sem, 1)
                if M:
                    for n in range(2, 4):
                        gated(m, n)
                if A:
                    hT = bx[0:TP, 0:NT * 128].rearrange("p (j b c) -> p b j c", j=NT, b=2)
                    wait(dve, HT, HT.at(1, a))
                    wait(dve, AT, AT.at("plus_v", a))
                    wait(dve, EO, EO.at("sum", a - 2))
                    V.tensor_tensor(h2[:, 1 - slot, :, :].rearrange("p (b j) c -> p b j c", b=2),
                                    hT, att_v[:, :, :].rearrange("p (b j) c -> p b j c", b=2),
                                    ALU.add).then_inc(AT.sem, 1)
                    wait(dve, AT, AT.at("h2", a))
                    for g in range(G):
                        i = V.bn_stats(st2[:, g, :], h2[:, 1 - slot, g, :])
                    i.then_inc(L2.sem, 1)
                    wait(dve, L2, L2.at("stats", a))
                    V.tensor_tensor(ln2[:, 0, :], st2[:, :, 1], st2[:, :, 4], ALU.subtract
                                    ).then_inc(L2.sem, 1)
                    V.tensor_tensor(ln2[:, 1, :], st2[:, :, 1], st2[:, :, 4], ALU.add
                                    ).then_inc(L2.sem, 1)
                    V.tensor_tensor(ln2[:, 2, :], st2[:, :, 2], st2[:, :, 5], ALU.add
                                    ).then_inc(L2.sem, 1)
                    wait(dve, L2, L2.at("dm", a))
                    V.tensor_tensor(ln2[:, 3, :], ln2[:, 0, :], ln2[:, 0, :], ALU.mult
                                    ).then_inc(L2.sem, 1)
                    wait(dve, L2, L2.at("dm2", a))
                    V.scalar_tensor_tensor(out=ln2[:, 4, :], in0=ln2[:, 3, :], scalar=C / 4.0,
                                           in1=ln2[:, 2, :], op0=ALU.mult, op1=ALU.add
                                           ).then_inc(L2.sem, 1)
                    wait(dve, L2, L2.at("var", a))
                    V.tensor_scalar(ln2[:, 5, :], ln2[:, 4, :], 1.0 / C, EPS_LAYER, ALU.mult,
                                    ALU.add).then_inc(L2.sem, 1)
                if F:
                    wait(dve, L1, L1.at("square", f))
                    V.tensor_reduce(ln1[:, 0, :].rearrange("p (b j) -> p j b", b=2),
                                    sq1[:, :, :, :], AX, ALU.add).then_inc(L1.sem, 1)
                    wait(dve, L1, L1.at("sum", f))
                    V.tensor_scalar(ln1[:, 1, :], ln1[:, 0, :], 1.0 / C, EPS_LAYER, ALU.mult,
                                    ALU.add).then_inc(L1.sem, 1)
                    wait(dve, L1, L1.at("rstd", f))
                    V.tensor_tensor(
                        t1[:, :, :].rearrange("p (b j) c -> p b j c", b=2),
                        bt[0:TP, 0:NT * 128].rearrange("p (j b c) -> p b j c", j=NT, b=2),
                        ln1[:, 2, :].rearrange("p (b j) -> p b j", b=2).unsqueeze(3)
                        .to_broadcast([TP, 2, NT, C]), ALU.mult).then_inc(L1.sem, 1)
                    wait(dve, L1, L1.at("norm", f))
                    V.tensor_copy(hl1[:, :, 0, :], t1[:, :, :]).then_inc(L1.sem, 1)
                if A:
                    wait(dve, L2, L2.at("rstd", a))
                    V.tensor_scalar(ln2[:, 7, :], ln2[:, 1, :], 0.5, None, ALU.mult
                                    ).then_inc(L2.sem, 1)
                    wait(dve, L2, L2.at("mean", a))
                    V.tensor_tensor(t2[:, :, :], h2[:, 1 - slot, :, :], per_token(ln2[:, 7, :]),
                                    ALU.subtract).then_inc(L2.sem, 1)
                    wait(dve, L2, L2.at("centred", a))
                    V.tensor_tensor(t2[:, :, :], t2[:, :, :], per_token(ln2[:, 6, :]),
                                    ALU.mult).then_inc(L2.sem, 1)
                    wait(dve, L2, L2.at("norm", a))
                    V.tensor_copy(hl2[:, :, 0, :], t2[:, :, :]).then_inc(L2.sem, 1)
                if M:
                    for n in range(4, 6):
                        gated(m, n)
                    wait(dve, EO, EO.at("product", m))
                    if not isinstance(s, int) or s >= 4:
                        dve.wait_ge(stored[slot], 16 * (m - slot))
                    V.tensor_tensor(y_out[:, slot, :, :], h2[:, slot, :, :],
                                    bt[0:TP, 0:G * C].rearrange("p (g c) -> p g c", g=G), ALU.add
                                    ).then_inc(EO.sem, 1)

            steps(dve, step)


def kernel(**inputs):
    import numpy as np
    import concourse.bacc as bacc
    from concourse.bass_utils import run_bass_kernel_spmd

    x = inputs["x"]
    B, TIN, C = x.shape
    w = {n.split("_", 2)[2]: np.asarray(a) for n, a in inputs.items() if n != "x"}
    E, _, H = w["expert_w1"].shape
    RH = w["router_w1"].shape[1]
    TAPS = w["w"].shape[0]
    J = E // 2
    blocks = np.kron(np.eye(2), np.ones((C, C))) / C
    pick = np.zeros((2 * E, J, 128))
    for e in range(E):
        for part in range(2):
            pick[e + part * E, e // 2, (e % 2) * C:(e % 2 + 1) * C] = 1.0
    const = {"squares": np.stack([np.eye(128), np.eye(128) - blocks, blocks], 1),
             "rank": np.tile(np.arange(E, 0, -1), (128, 1)), "pick": pick}

    def twice(a):
        return np.concatenate([a, a], 0)

    q, k, v = np.split(w["W_qkv"], 3, 1)
    bq, bk, bv = np.split(w["b_qkv"], 3)
    w1 = w["expert_w1"].transpose(1, 0, 2).reshape(C, E * H)
    columns = [twice(w["w"].reshape(TAPS, C).T)]
    columns += [twice(a[:, None]) for a in (w["b"], w["gamma"], w["beta"], w["alpha"], w["b_out"], bq)]
    columns += [w["expert_b1"].reshape(J, 128).T, w["expert_b2"].reshape(J, 128).T]
    columns += [np.concatenate([w["router_b1"], np.zeros(128 - RH, np.float32)])[:, None]]
    w2 = np.zeros((2, H, J, 2, H), np.float32)
    for a in range(2):
        w2[a, :, :, a, :] = w["expert_w2"][a::2].transpose(1, 0, 2)
    laid = {
        "stack": twice(np.concatenate([q, q, k, v, w1, w["router_w1"]], 1)),
        "head": np.concatenate([v.T, v.T, w["W_out"], bv[:, None]], 1),
        "b_k": bk[None], "b3": twice(w["expert_b3"]),
        "wr2": np.concatenate([w["router_w2"], w["router_b2"][None]], 0),
        "w3": w["expert_w3"].reshape(J, 128, C).transpose(1, 0, 2),
        "w2": w2.reshape(128, J, 128), "cols": np.concatenate(columns, 1),
    }
    nc = bacc.Bacc("TRN2", target_bir_lowering=False, num_devices=1)
    arrays = {}

    def given(name, a):
        a = np.ascontiguousarray(a)
        arrays[name] = a
        return nc.dram_tensor(name, a.shape, mybir.dt.from_np(a.dtype), kind="ExternalInput").ap()

    xs = given("x_dram", x)
    ws = {n: given(f"{n}_dram", a) for n, a in laid.items()}
    cs = {n: given(f"{n}_const", a.astype(np.float32)) for n, a in const.items()}
    out = nc.dram_tensor("out_dram", (B, TIN // 2, C), F32, kind="ExternalOutput").ap()
    audio_tower(nc, xs, ws, cs, out, E, H, RH, TAPS)
    r = run_bass_kernel_spmd(nc, [arrays], core_ids=[0])
    return r.results[0]["out_dram"]
```

```python
from contextlib import ExitStack

import concourse.bass as bass
from concourse import mybir

F32 = mybir.dt.float32
F16 = mybir.dt.float16
ALU = mybir.AluOpType
ACT = mybir.ActivationFunctionType
AX = mybir.AxisListType.X

EPS_BATCH = 1e-3
EPS_LAYER = 1e-5
EPS_DIV = 1e-7
EPS_NORM = 1e-12


class Chain:

    def __init__(self, sem, steps):
        self.sem = sem
        self.steps = {name: n + 1 for n, name in enumerate(steps.split())}

    def at(self, step, pair):
        return len(self.steps) * pair + self.steps[step]


class Count:

    def __init__(self, sem, per):
        self.sem, self.per = sem, per

    def at(self, n, pair):
        return self.per * pair + n


def audio_tower(nc, x, w, const, out, E, H, RH, TAPS):
    B, TIN, C = x.shape
    T = out.shape[1]
    PAIRS = B // 2
    P = 2 * C
    NT = 3
    TP = T // NT
    G = 2 * NT
    J = E // 2
    TE = TP + TP % 2
    NX = TIN // TP
    assert P == 128 and C == H and T == NT * TP and TIN == 2 * T and TAPS == 5 and B % 4 == 0

    Q0, K0, V0, E0, R0 = 0, P, P + C, P + 2 * C, P + 2 * C + E * H
    WCOLS = R0 + RH

    with ExitStack() as ctx:
        def sb(name, shape, dt=F32):
            return ctx.enter_context(nc.sbuf_tensor(name, shape, dt))

        def bank(name, dt=F32):
            return ctx.enter_context(nc.psum_tensor(name, [128, 512 if dt == F32 else 1024], dt))

        def sem(name):
            return ctx.enter_context(nc.semaphore(name))

        const_in = sb("const_in", [128, 3, 128])
        ident, centre, average = (const_in[:, i, :] for i in range(3))
        ident16 = sb("ident16", [128, 128], F16)
        pick_in = sb("pick_in", [2 * E, J, 128])
        pick = sb("pick", [2 * E, J, 128], F16)
        rank = sb("rank", [128, E])
        minus_half = sb("minus_half", [128, G])
        stack = sb("stack", [128, WCOLS])
        stack_hi = sb("stack_hi", [128, WCOLS], F16)
        stack_lo = sb("stack_lo", [128, WCOLS], F16)
        head = sb("head", [C, 3 * C + 1])
        wvT, wout, bv = head[:, 0:2 * C], head[:, 2 * C:3 * C], head[:, 3 * C:]
        row_mean = sb("row_mean", [128, 4])
        bqc = sb("bqc", [128, 1])
        kv_row = sb("kv_row", [1, 2, C])
        kv_lo = sb("kv_lo", [1, NT, 2 * C], F16)
        kv_bias = sb("kv_bias", [2, NT, 2 * C], F16)
        ones2 = sb("ones2", [2, TP], F16)
        w2 = sb("w2", [128, J, 128])
        w3 = sb("w3", [128, J, C])
        b3 = sb("b3", [2 * E, C])
        b3_hi = sb("b3_hi", [2 * E, C], F16)
        b3_lo = sb("b3_lo", [2 * E, C], F16)
        wr2 = sb("wr2", [RH + 1, E])
        cols = sb("cols", [128, TAPS + 6 + 2 * J + 1])
        conv_w = cols[:, 0:TAPS]
        conv_b, gamma, beta, alpha, b_out, bq = (cols[:, TAPS + i:TAPS + i + 1] for i in range(6))
        b1 = cols[:, TAPS + 6:TAPS + 6 + J]
        b2 = cols[:, TAPS + 6 + J:TAPS + 6 + 2 * J]
        br1 = cols[0:RH, TAPS + 6 + 2 * J:]
        negative = sb("negative", [128, 2])

        x_in = sb("x_in", [TP, 2, NX, 2, C])
        xT = sb("xT", [128, TIN + 4])
        y = sb("y", [128, T])
        stats = sb("stats", [128, 6])
        bn = sb("bn", [128, 12])
        above = sb("above", [128, NT, TP])
        below = sb("below", [128, NT, TP])
        h = sb("h", [128, NT, TP])
        hb = sb("hb", [128, 2, NT, TP])
        sq1 = sb("sq1", [TP, NT, 2, C])
        ln1 = sb("ln1", [TP, 3, G])
        t1 = sb("t1", [TP, G, C])
        hl1 = sb("hl1", [TP, G, 2, C], F16)
        l1 = sb("l1", [128, G, TP], F16)
        k_sq = sb("k_sq", [TP, G, C])
        ks = sb("ks", [TP, 3, G])
        kk = sb("kk", [TP, G, 2, C])
        v1 = sb("v1", [TP, 2, G, C + 1])
        q2 = sb("q2", [128, G, TP])
        kn = sb("kn", [C, 3, 2])
        kvn = sb("kvn", [128, 2, C + 2])
        at = sb("at", [TP, 8, G])
        att = sb("att", [TP, G, C])
        att_v = sb("att_v", [TP, G, C])
        h2 = sb("h2", [TP, 2, G, C])
        st2 = sb("st2", [TP, G, 6])
        ln2 = sb("ln2", [TP, 8, G])
        t2 = sb("t2", [TP, G, C])
        hl2 = sb("hl2", [TP, G, 2, C], F16)
        l2 = sb("l2", [128, G, TP], F16)
        rh = sb("rh", [RH + 1, G, TP])
        rt = sb("rt", [TP, 9, G, E])
        rs = sb("rs", [TP, 10, G])
        gate = sb("gate", [TP, G, 2, E], F16)
        gateT = sb("gateT", [2 * E, 2, G, TP], F16)
        e1 = sb("e1", [128, J, G, TP])
        e2 = sb("e2", [128, J, G, TP])
        e2g = sb("e2g", [128, J, G, TP])
        e_out = sb("e_out", [TP, G, C])
        y_out = sb("y_out", [TP, 2, G, C])

        bx = bank("bx")
        bk = [bank(f"bk{b}") for b in range(2)]
        bt = bank("bt")
        bl = bank("bl", F16)
        bs = bank("bs")
        bh = [bank(f"bh{i}") for i in range(2)]

        s_w = sem("weights_in")
        s_b = sem("low_bias_moved")
        SET = Chain(sem("setup"), "vw vwc bq bqc mean scaled centred bias hilo all")
        s_set = SET.sem
        s_fill = sem("filled")
        carrier = sem("carrier")
        x_ready = [sem(f"x_ready{i}") for i in range(2)]
        stored = [sem(f"stored{i}") for i in range(2)]

        XT = Chain(sem("x_turned"), "turn0 copy0 turn1 copy1")
        BN = Chain(sem("front"), "tap0 tap1 tap2 tap3 tap4 stats aggr mean dev var_c var var_eps"
                   " rstd scale nscale shift0 shift nshift above below prelu")
        HB = Count(sem("h_biased"), 1)
        L1 = Chain(sem("layer_norm_1"), "centred square sum var rstd norm high low turn copy")
        KP = Count(sem("kv_product"), 2)
        KE = Count(sem("kv_taken"), 4)
        KN = Chain(sem("k_normed"), "sum eps recip k2 k4 kv least rlen kvn0 kvn1")
        QC = Chain(sem("q_squared"), "q0 sq0 q1 sq1 q4")
        HT = Count(sem("h_turned"), 1)
        AT = Chain(sem("attention"), "t2 eps recip n1 n2 least rlen scale scaled plus_v h2")
        L2 = Chain(sem("layer_norm_2"), "stats dm sm m2 dm2 var mean var_eps rstd norm"
                   " high low turn copy")
        CE = Count(sem("centred_2"), 1)
        RP = Count(sem("router_product"), 2)
        RA = Count(sem("router_relu"), 2)
        RT = Chain(sem("routing"), "logits max shifted exp sum recip marked1 first1 one1 rest max2"
                   " e2 gap0 marked2 first2 one2 diff gap egap egap1 w1 part gates high low turn"
                   " copy")
        E1P, E1A = Count(sem("expert1_product"), 2 * J), Count(sem("expert1_relu"), 2 * J)
        E2P, E2A = Count(sem("expert2_product"), 2 * J), Count(sem("expert2_relu"), 2 * J)
        GP, GA = Count(sem("gates_spread"), 2 * J), Count(sem("gated"), 2 * J)
        EO = Chain(sem("experts_out"), "product0 product1 copy")
        YS = Count(sem("residual_added"), 1)
        YR = Count(sem("residual_copied"), 1)

        weight_loads = [
            (const_in[:, :, :], const["squares"]), (cols[:, :], w["cols"]),
            (stack[:, :], w["stack"]), (head[:, :], w["head"]), (kv_row[:, 0, :], w["b_k"]),
            (pick_in[:, :, :], const["pick"]), (rank[:, :], const["rank"]),
            (b3[:, :], w["b3"]), (wr2[:, :], w["wr2"]), (w3[:, :, :], w["w3"]),
            (w2[:, :, :], w["w2"]),
        ]

        block = ctx.enter_context(nc.Block())

        def loaded(pair, slot):
            return 16 * (pair - slot) + 32

        def steps(eng, run):
            def peeled(s):
                run(s, s % 2, [0 <= s - stage < PAIRS for stage in range(5)])

            first = 6
            for s in range(first):
                peeled(s)
            with eng.Fori(first // 2, PAIRS // 2) as half:
                for parity in range(2):
                    run(2 * half + parity, parity, [True] * 5)
            for s in range(PAIRS, PAIRS + 4):
                peeled(s)

        def worked(pair):
            return not isinstance(pair, int) or 0 <= pair < PAIRS

        @block.sync
        def _(sp):
            def load(pair, slot):
                for b in range(2):
                    sp.dma_start(x_in[:, slot, :, b, :],
                                 x[bass.ds(2 * pair + b, 1)].rearrange("o (p j) c -> p (o j) c", j=NX)
                                 ).then_inc(x_ready[slot], 16)

            load(0, 0)
            load(1, 1)
            for dst, src in weight_loads[0::2]:
                sp.dma_start(dst, src).then_inc(s_w, 16)

            def step(s, slot):
                if worked(s):
                    if worked(s - 2):
                        sp.wait_ge(XT.sem, XT.at("turn1", s - 2))
                    load(s, slot)
                if worked(s - 5):
                    if worked(s - 5):
                        sp.wait_ge(YS.sem, YS.at(1, s - 5))
                    for b in range(2):
                        sp.dma_start(
                            out[bass.ds(2 * (s - 5) + b, 1)].rearrange("o (p j) c -> p (o j) c", j=NT),
                            y_out[:, 1 - slot, b * NT:(b + 1) * NT, :]).then_inc(stored[1 - slot], 16)

            for s in range(2, 6):
                step(s, s % 2)
            with sp.Fori(3, PAIRS // 2) as half:
                for parity in range(2):
                    step(2 * half + parity, parity)
            for s in range(PAIRS, PAIRS + 5):
                step(s, s % 2)
            for slot in range(2):
                sp.wait_ge(stored[slot], 16 * PAIRS)

        @block.gpsimd
        def _(pool):
            pool.wait_ge(SET.sem, SET.at("hilo", 0))
            pool.dma_start(kv_bias[1:2, :, :], kv_lo[:, :, :]).then_inc(s_b, 16)
            pool.wait_ge(SET.sem, SET.at("all", 0))

            def step(s, slot, at_work):
                F, A, B_, M, N = at_work
                f, a, b, m, n = s, s - 1, s - 2, s - 3, s - 4
                if B_:
                    pool.wait_ge(AT.sem, AT.at("least", b))
                    nc.gpsimd.tensor_tensor(at[:, 5, :], at[:, 4, :], minus_half[0:TP, :],
                                            ALU.pow).then_inc(AT.sem, 1)
                if M:
                    pool.wait_ge(AT.sem, AT.at("h2", m))
                    if worked(m - 2):
                        pool.wait_ge(stored[1 - slot], 16 * (m - 2 - (1 - slot)) + 32)
                    pool.sem_inc(carrier)
                    nc.gpsimd.tensor_copy(y_out[:, 1 - slot, :, :], h2[:, 1 - slot, :, :]
                                          ).then_inc(YR.sem, 1)
                if B_:
                    pool.wait_ge(AT.sem, AT.at("scaled", b))
                    nc.gpsimd.tensor_tensor(att_v[:, :, :], att[:, :, :], v1[:, slot, :, 0:C],
                                            ALU.add).then_inc(AT.sem, 1)
                if A:
                    pool.wait_ge(KN.sem, KN.at("k2", a))
                    nc.gpsimd.tensor_tensor(kk[:, :, 1, :], kk[:, :, 0, :], kk[:, :, 0, :],
                                            ALU.mult).then_inc(KN.sem, 1)
                if F:
                    pool.wait_ge(BN.sem, BN.at("var_eps", f))
                    nc.gpsimd.tensor_tensor(bn[:, 5:6], bn[:, 4:5], minus_half[:, 0:1],
                                            ALU.pow).then_inc(BN.sem, 1)
                if A:
                    pool.wait_ge(KN.sem, KN.at("least", a))
                    if F:
                        pool.wait_ge(BN.sem, BN.at("rstd", f))
                    nc.gpsimd.tensor_tensor(kn[:, 1, :], kn[:, 0, :], minus_half[0:C, 0:2],
                                            ALU.pow).then_inc(KN.sem, 1)
                if B_:
                    pool.wait_ge(L2.sem, L2.at("var_eps", b))
                    if A:
                        pool.wait_ge(KN.sem, KN.at("rlen", a))
                    nc.gpsimd.tensor_tensor(ln2[:, 6, :], ln2[:, 5, :], minus_half[0:TP, :],
                                            ALU.pow).then_inc(L2.sem, 1)
                if A:
                    pool.wait_ge(QC.sem, QC.at("sq1", a))
                    pool.wait_ge(KN.sem, KN.at("rlen", a))
                    if B_:
                        pool.wait_ge(L2.sem, L2.at("rstd", b))
                    nc.gpsimd.tensor_tensor(q2[C:2 * C, :, :], q2[C:2 * C, :, :], q2[C:2 * C, :, :],
                                            ALU.mult).then_inc(QC.sem, 1)
                if B_:
                    pool.wait_ge(L2.sem, L2.at("high", b))
                    if A:
                        pool.wait_ge(QC.sem, QC.at("q4", a))
                    nc.gpsimd.tensor_tensor(hl2[:, :, 1, :], t2[:, :, :], hl2[:, :, 0, :],
                                            ALU.subtract).then_inc(L2.sem, 1)
                if F:
                    pool.wait_ge(L1.sem, L1.at("var", f))
                    if A:
                        pool.wait_ge(QC.sem, QC.at("q4", a))
                    nc.gpsimd.tensor_tensor(ln1[:, 2, :], ln1[:, 1, :], minus_half[0:TP, :],
                                            ALU.pow).then_inc(L1.sem, 1)
                    pool.wait_ge(L1.sem, L1.at("high", f))
                    nc.gpsimd.tensor_tensor(hl1[:, :, 1, :], t1[:, :, :], hl1[:, :, 0, :],
                                            ALU.subtract).then_inc(L1.sem, 1)
                if N:
                    pool.wait_ge(YR.sem, YR.at(1, n))
                    pool.wait_ge(EO.sem, EO.at("copy", n))
                    nc.gpsimd.tensor_tensor(y_out[:, slot, :, :], y_out[:, slot, :, :],
                                            e_out[:, :, :], ALU.add).then_inc(YS.sem, 1)

            steps(pool, step)

        @block.tensor
        def _(pe):
            n_w = 16 * len(weight_loads)
            pe.wait_ge(s_w, n_w)
            nc.tensor.matmul(bs[:, 0:C], wvT, wout, start=True, stop=True)
            nc.tensor.matmul(bx[0:1, 0:C], bv, wout, start=True, stop=True
                             ).then_inc(s_set, 1)
            pe.wait_ge(s_set, SET.at("vwc", 0))
            nc.tensor.matmul(bs[:, 0:1], centre, bq, start=True, stop=True
                             ).then_inc(s_set, 1)
            pe.wait_ge(s_set, SET.at("all", 0))
            pe.wait_ge(s_b, 16)
            pe.wait_ge(s_fill, 8)

            def turn_split(bank_, hl, chain):
                for g in range(G):
                    i = nc.tensor.transpose(bank_[:, g * TE:g * TE + TP],
                                            hl[:, g, :, :].rearrange("p a c -> p (a c)"),
                                            ident16[0:TP, 0:TP])
                i.then_inc(chain.sem, 1)

            def split_product(dst, l, col, n, b):
                rhs = l[:, b * NT:(b + 1) * NT, :]
                nc.tensor.matmul(dst, stack_hi[:, col:col + n], rhs, start=True, stop=False)
                return nc.tensor.matmul(dst, stack_lo[:, col:col + n], rhs, start=False, stop=True)

            def expert1(m, i, N):
                j, b = i // 2, i % 2
                if i >= 2:
                    pe.wait_ge(E1A.sem, E1A.at(i - 1, m))
                elif N:
                    if worked(m - 1):
                        pe.wait_ge(E2A.sem, E2A.at(2 * J - 1 + i, m - 1))
                split_product(bh[i % 2][:, 0:T], l2, E0 + j * 128, 128, b).then_inc(E1P.sem, 1)

            def expert2(n, i):
                j, b = i // 2, i % 2
                if i < 2:
                    pe.wait_ge(E1A.sem, E1A.at(2 * J - 1 + i, n))
                else:
                    pe.wait_ge(E2A.sem, E2A.at(i - 1, n))
                nc.tensor.matmul(bh[i % 2][:, 0:T], w2[:, j, :], e1[:, j, b * NT:(b + 1) * NT, :],
                                 start=True, stop=True).then_inc(E2P.sem, 1)

            def spread(n, slot, A, M, i):
                j, b = i // 2, i % 2
                if i >= 2:
                    pe.wait_ge(GA.sem, GA.at(i - 1, n))
                elif A:
                    pe.wait_ge(KE.sem, KE.at(2 * i + 2, n + 3))
                elif M:
                    pe.wait_ge(RA.sem, RA.at(i + 1, n + 1))
                else:
                    if worked(n - 1):
                        pe.wait_ge(GA.sem, GA.at(2 * J - 1 + i, n - 1))
                if i == 0:
                    pe.wait_ge(RT.sem, RT.at("copy", n))
                nc.tensor.matmul(bk[i % 2][:, 0:T], pick[:, j, :],
                                 gateT[:, slot, b * NT:(b + 1) * NT, :],
                                 start=True, stop=True).then_inc(GP.sem, 1)

            def turn_x(f, slot, half):
                for j in range(NX // 2):
                    i = nc.tensor.transpose(
                        bx[:, j * TP:(j + 1) * TP],
                        x_in[:, slot, half * NX // 2 + j, :, :].rearrange("p b c -> p (b c)"),
                        ident[0:TP, 0:TP])
                i.then_inc(XT.sem, 1)

            def router_hidden(m, h_):
                if h_ == 0:
                    pe.wait_ge(L2.sem, L2.at("copy", m))
                if worked(m - 2):
                    pe.wait_ge(GA.sem, GA.at(2 * J - 1 + h_, m - 2))
                else:
                    pe.wait_ge(KE.sem, KE.at(2 * h_ + 2, m + 1))
                split_product(bk[h_][0:RH, 0:T], l2, R0, RH, h_).then_inc(RP.sem, 1)

            def keys_values(a, M, h_):
                if h_ == 0:
                    pe.wait_ge(L1.sem, L1.at("copy", a))
                if M:
                    pe.wait_ge(RA.sem, RA.at(h_ + 1, a - 2))
                else:
                    if worked(a - 1):
                        pe.wait_ge(KE.sem, KE.at(2 * h_ + 2, a - 1))
                nc.tensor.matmul(bk[h_][0:TP, 0:NT * 2 * C], ones2[:, :], kv_bias[:, :, :],
                                 start=True, stop=False, skip_group_check=True)
                for j in range(NT):
                    dst = bk[h_][0:TP, j * 2 * C:(j + 1) * 2 * C]
                    nc.tensor.matmul(dst, l1[:, h_ * NT + j, :], stack_hi[:, K0:E0],
                                     start=False, stop=False, skip_group_check=True)
                    i = nc.tensor.matmul(dst, l1[:, h_ * NT + j, :], stack_lo[:, K0:E0],
                                         start=False, stop=j == NT - 1, skip_group_check=True)
                i.then_inc(KP.sem, 1)

            def queries(a, F, h_):
                if h_ == 1:
                    pe.wait_ge(QC.sem, QC.at("sq0", a))
                elif F:
                    pe.wait_ge(XT.sem, XT.at("copy1", a + 1))
                else:
                    pe.wait_ge(L1.sem, L1.at("norm", a))
                split_product(bx[:, 0:T], l1, Q0, 128, h_).then_inc(QC.sem, 1)

            def third_layers(n, slot, B_, half):
                pe.wait_ge(GA.sem, GA.at(2 * J - 1 + half, n))
                if half == 0:
                    if B_:
                        pe.wait_ge(AT.sem, AT.at("scaled", n + 2))
                    elif worked(n - 1):
                        pe.wait_ge(EO.sem, EO.at("copy", n - 1))
                for g in range(half * NT, (half + 1) * NT):
                    dst = bt[0:TP, g * C:(g + 1) * C]
                    nc.tensor.matmul(dst, gateT[:, slot, g, :], b3_hi[:, :],
                                     start=True, stop=False)
                    nc.tensor.matmul(dst, gateT[:, slot, g, :], b3_lo[:, :],
                                     start=False, stop=False)
                    for j in range(J):
                        i = nc.tensor.matmul(dst, e2g[:, j, g, :], w3[:, j, :],
                                             start=False, stop=j == J - 1)
                i.then_inc(EO.sem, 1)

            def step(s, slot, at_work):
                F, A, B_, M, N = at_work
                f, a, b, m, n = s, s - 1, s - 2, s - 3, s - 4
                if N:
                    expert2(n, 0)
                if M:
                    pe.wait_ge(L2.sem, L2.at("low", m))
                    if worked(m - 1):
                        pe.wait_ge(RT.sem, RT.at("copy", m - 1))
                    else:
                        pe.wait_ge(L1.sem, L1.at("copy", m + 1))
                    turn_split(bl, hl2, L2)
                if F:
                    pe.wait_ge(x_ready[slot], loaded(f, slot))
                    if worked(f - 1):
                        pe.wait_ge(L1.sem, L1.at("norm", f - 1))
                    turn_x(f, slot, 0)
                if M:
                    router_hidden(m, 0)
                if F:
                    pe.wait_ge(XT.sem, XT.at("copy0", f))
                    turn_x(f, slot, 1)
                if B_:
                    pe.wait_ge(QC.sem, QC.at("q4", b))
                    pe.wait_ge(KN.sem, KN.at("kvn1", b))
                    if worked(n - 1):
                        pe.wait_ge(EO.sem, EO.at("copy", n - 1))
                    else:
                        if worked(b - 1):
                            pe.wait_ge(AT.sem, AT.at("scaled", b - 1))
                    for g in range(G):
                        i = nc.tensor.matmul(bt[0:TP, g * (C + 2):(g + 1) * (C + 2)], q2[:, g, :],
                                             kvn[:, g // NT, :], start=True, stop=True)
                    i.then_inc(AT.sem, 1)
                if A:
                    pe.wait_ge(L1.sem, L1.at("low", a))
                    if M:
                        pe.wait_ge(L2.sem, L2.at("copy", m))
                    else:
                        if worked(a - 1):
                            pe.wait_ge(L1.sem, L1.at("copy", a - 1))
                    turn_split(bl, hl1, L1)
                if M:
                    router_hidden(m, 1)
                if N:
                    expert2(n, 1)
                if A:
                    keys_values(a, M, 0)
                if M:
                    pe.wait_ge(RA.sem, RA.at(2, m))
                    if worked(s - 2):
                        pe.wait_ge(KN.sem, KN.at("kvn1", s - 2))
                    else:
                        if worked(m - 1):
                            pe.wait_ge(RT.sem, RT.at("shifted", m - 1))
                    for g in range(G):
                        i = nc.tensor.matmul(bs[0:TP, g * E:(g + 1) * E], rh[:, g, :], wr2[:, :],
                                             start=True, stop=True)
                    i.then_inc(RT.sem, 1)
                if N:
                    expert2(n, 2)
                if A:
                    keys_values(a, M, 1)
                if N:
                    spread(n, slot, A, M, 0)
                    expert2(n, 3)
                if A:
                    queries(a, F, 0)
                if N:
                    expert2(n, 4)
                    spread(n, slot, A, M, 1)
                if A:
                    queries(a, F, 1)
                if F:
                    pe.wait_ge(BN.sem, BN.at("aggr", f))
                    if M:
                        pe.wait_ge(RT.sem, RT.at("shifted", m))
                    if worked(f - 2):
                        pe.wait_ge(KN.sem, KN.at("kvn1", f - 2))
                    nc.tensor.matmul(bs[:, 0:1], average, bn[:, 0:1], start=True, stop=True
                                     ).then_inc(BN.sem, 1)
                if N:
                    expert2(n, 5)
                if B_:
                    pe.wait_ge(HB.sem, HB.at(1, b))
                    if A:
                        pe.wait_ge(QC.sem, QC.at("sq1", a))
                    else:
                        if worked(b - 1):
                            pe.wait_ge(AT.sem, AT.at("h2", b - 1))
                    for j in range(NT):
                        i = nc.tensor.transpose(bx[0:TP, j * 128:(j + 1) * 128], hb[:, slot, j, :],
                                                ident)
                    i.then_inc(HT.sem, 1)
                if N:
                    spread(n, slot, A, M, 2)
                if F:
                    pe.wait_ge(BN.sem, BN.at("var_c", f))
                    nc.tensor.matmul(bs[:, 1:2], average, bn[:, 3:4], start=True, stop=True
                                     ).then_inc(BN.sem, 1)
                if M:
                    expert1(m, 0, N)
                if N:
                    spread(n, slot, A, M, 3)
                if M:
                    expert1(m, 1, N)
                if N:
                    spread(n, slot, A, M, 4)
                if M:
                    expert1(m, 2, N)
                if N:
                    spread(n, slot, A, M, 5)
                if M:
                    expert1(m, 3, N)
                if A:
                    pe.wait_ge(KN.sem, KN.at("k4", a))
                    pe.wait_ge(KE.sem, KE.at(4, a))
                    if F:
                        pe.wait_ge(BN.sem, BN.at("shift0", f))
                    elif M:
                        pe.wait_ge(RT.sem, RT.at("shifted", m))
                    for h_ in range(2):
                        for j in range(NT):
                            g = h_ * NT + j
                            i = nc.tensor.matmul(bs[:, h_ * (C + 1):(h_ + 1) * (C + 1)],
                                                 kk[:, g, :, :], v1[:, 1 - slot, g, :],
                                                 start=j == 0, stop=j == NT - 1)
                    i.then_inc(KN.sem, 1)
                if N:
                    third_layers(n, slot, B_, 0)
                if M:
                    expert1(m, 4, N)
                if F:
                    pe.wait_ge(BN.sem, BN.at("prelu", f))
                    if B_:
                        pe.wait_ge(AT.sem, AT.at("h2", b))
                    elif A:
                        pe.wait_ge(QC.sem, QC.at("sq1", a))
                    for j in range(NT):
                        i = nc.tensor.matmul(bx[0:TP, j * 128:(j + 1) * 128], h[:, j, :],
                                             centre, start=True, stop=True)
                    i.then_inc(L1.sem, 1)
                if N:
                    third_layers(n, slot, B_, 1)
                if M:
                    pe.wait_ge(RT.sem, RT.at("low", m))
                    if A:
                        pe.wait_ge(L1.sem, L1.at("copy", a))
                    else:
                        pe.wait_ge(L2.sem, L2.at("copy", m))
                    for g in range(G):
                        i = nc.tensor.transpose(bl[0:2 * E, g * TE:g * TE + TP],
                                                gate[:, g, :, :].rearrange("p a e -> p (a e)"),
                                                ident16[0:TP, 0:TP])
                    i.then_inc(RT.sem, 1)
                    expert1(m, 5, N)

            steps(pe, step)

        @block.scalar
        def _(act):
            for dst, src in weight_loads[1::2]:
                act.dma_start(dst, src).then_inc(s_w, 16)
            act.wait_ge(s_set, SET.at("all", 0))
            act.wait_ge(s_fill, 8)

            def expert_relu(P_, A_, dst, bias, pair, i):
                j, b = i // 2, i % 2
                act.wait_ge(P_.sem, P_.at(i + 1, pair))
                nc.scalar.activation(dst[:, j, b * NT:(b + 1) * NT, :],
                                     bh[i % 2][:, 0:T].rearrange("p (j t) -> p j t", j=NT),
                                     ACT.Relu, bias=bias[:, j:j + 1]).then_inc(A_.sem, 1)

            def relu1(m, i):
                if i == 0:
                    if worked(m - 1):
                        act.wait_ge(E2P.sem, E2P.at(2 * J, m - 1))
                expert_relu(E1P, E1A, e1, b1, m, i)

            def relu2(n, i):
                if i == 0:
                    if worked(n - 1):
                        act.wait_ge(GA.sem, GA.at(2 * J, n - 1))
                expert_relu(E2P, E2A, e2, b2, n, i)

            def copy_x(f, half):
                act.wait_ge(XT.sem, XT.at(f"turn{half}", f))
                if half == 0:
                    if worked(f - 1):
                        act.wait_ge(BN.sem, BN.at("tap4", f - 1))
                dst = xT[:, 1:1 + TIN].rearrange("p (t j) -> p j t", j=NX)
                nc.scalar.activation(dst[:, half * NX // 2:(half + 1) * NX // 2, :],
                                     bx[:, 0:T].rearrange("p (j t) -> p j t", j=NX // 2),
                                     ACT.Copy).then_inc(XT.sem, 1)

            def router_relu(m, h_):
                act.wait_ge(RP.sem, RP.at(h_ + 1, m))
                if h_ == 0:
                    if worked(m - 1):
                        act.wait_ge(RT.sem, RT.at("logits", m - 1))
                nc.scalar.activation(rh[0:RH, h_ * NT:(h_ + 1) * NT, :],
                                     bk[h_][0:RH, 0:T].rearrange("p (j t) -> p j t", j=NT),
                                     ACT.Relu, bias=br1).then_inc(RA.sem, 1)

            def take_kv(a, slot, h_):
                kv = bk[h_][0:TP, 0:NT * 2 * C].rearrange("p (j c) -> p j c", j=NT)
                act.wait_ge(KP.sem, KP.at(h_ + 1, a))
                if h_ == 0:
                    if worked(a - 1):
                        act.wait_ge(KN.sem, KN.at("kv", a - 1))
                    if worked(a - 2):
                        act.wait_ge(AT.sem, AT.at("plus_v", a - 2))
                nc.scalar.activation(k_sq[:, h_ * NT:(h_ + 1) * NT, :], kv[:, :, 0:C],
                                     ACT.Square).then_inc(KE.sem, 1)
                nc.scalar.activation(v1[:, 1 - slot, h_ * NT:(h_ + 1) * NT, 0:C],
                                     kv[:, :, C:2 * C], ACT.Copy).then_inc(KE.sem, 1)

            def square_q(a, h_):
                act.wait_ge(QC.sem, QC.at(f"q{h_}", a))
                if h_ == 0:
                    if worked(a - 1):
                        act.wait_ge(AT.sem, AT.at("t2", a - 1))
                nc.scalar.activation(q2[:, h_ * NT:(h_ + 1) * NT, :],
                                     bx[:, 0:T].rearrange("p (j t) -> p j t", j=NT),
                                     ACT.Square, bias=bqc[:, :]).then_inc(QC.sem, 1)

            def step(s, slot, at_work):
                F, A, B_, M, N = at_work
                f, a, b, m, n = s, s - 1, s - 2, s - 3, s - 4
                if F:
                    copy_x(f, 0)
                if M:
                    router_relu(m, 0)
                if F:
                    copy_x(f, 1)
                    act.wait_ge(XT.sem, XT.at("copy1", f))
                    if worked(f - 1):
                        act.wait_ge(BN.sem, BN.at("below", f - 1))
                    nc.scalar.activation(y[:, :], xT[:, 0:2 * T:2], ACT.Identity, bias=conv_b,
                                         scale=conv_w[:, 0:1]).then_inc(BN.sem, 1)
                if A:
                    if worked(a - 1):
                        act.wait_ge(QC.sem, QC.at("q1", a - 1))
                    act.wait_ge(L1.sem, L1.at("turn", a))
                    nc.scalar.activation(l1[:, :, :], bl[:, 0:G * TE].rearrange(
                        "p (g t) -> p g t", g=G)[:, :, 0:TP], ACT.Copy).then_inc(L1.sem, 1)
                if M:
                    router_relu(m, 1)
                if N:
                    relu2(n, 0)
                if A:
                    take_kv(a, slot, 0)
                if N:
                    relu2(n, 1)
                if M:
                    act.wait_ge(RT.sem, RT.at("shifted", m))
                    nc.scalar.activation(rt[:, 1, :, :], rt[:, 0, :, :], ACT.Exp).then_inc(RT.sem, 1)
                if A:
                    take_kv(a, slot, 1)
                if N:
                    relu2(n, 2)
                if A:
                    square_q(a, 0)
                if N:
                    relu2(n, 3)
                if A:
                    square_q(a, 1)
                if N:
                    relu2(n, 4)
                    relu2(n, 5)
                if M:
                    relu1(m, 0)
                    relu1(m, 1)
                    relu1(m, 2)
                    act.wait_ge(RT.sem, RT.at("max2", m))
                    nc.scalar.activation(rs[:, 6, :], rs[:, 7, :], ACT.Exp).then_inc(RT.sem, 1)
                if F:
                    by_tile = y[:, :].rearrange("p (t j) -> p j t", j=NT)
                    act.wait_ge(BN.sem, BN.at("nshift", f))
                    nc.scalar.activation(above[:, :, :], by_tile, ACT.Relu, bias=bn[:, 8:9],
                                         scale=bn[:, 6:7]).then_inc(BN.sem, 1)
                if M:
                    relu1(m, 3)
                if F:
                    nc.scalar.activation(below[:, :, :], by_tile, ACT.Relu, bias=bn[:, 10:11],
                                         scale=bn[:, 9:10]).then_inc(BN.sem, 1)
                if M:
                    act.wait_ge(RT.sem, RT.at("gap", m))
                    nc.scalar.activation(rs[:, 2, :], rs[:, 5, :], ACT.Exp).then_inc(RT.sem, 1)
                    relu1(m, 4)
                if F:
                    act.wait_ge(L1.sem, L1.at("centred", f))
                    nc.scalar.activation(sq1[:, :, :, :].rearrange("p j b c -> p (j b c)"),
                                         bx[0:TP, 0:NT * 128], ACT.Square).then_inc(L1.sem, 1)
                if B_:
                    if worked(b - 1):
                        act.wait_ge(L2.sem, L2.at("turn", b - 1))
                    act.wait_ge(L2.sem, L2.at("norm", b))
                    nc.scalar.activation(hl2[:, :, 0, :], t2[:, :, :], ACT.Copy).then_inc(L2.sem, 1)
                if F:
                    if worked(f - 2):
                        act.wait_ge(HT.sem, HT.at(1, f - 2))
                    nc.scalar.activation(hb[:, slot, :, :], h[:, :, :], ACT.Identity, bias=b_out
                                         ).then_inc(HB.sem, 1)
                if N:
                    if worked(n - 1):
                        act.wait_ge(YS.sem, YS.at(1, n - 1))
                    act.wait_ge(EO.sem, EO.at("product1", n))
                    nc.scalar.activation(e_out[:, :, :], bt[0:TP, 0:G * C].rearrange(
                        "p (g c) -> p g c", g=G), ACT.Copy).then_inc(EO.sem, 1)
                if M:
                    relu1(m, 5)
                if F:
                    if worked(f - 1):
                        act.wait_ge(L1.sem, L1.at("turn", f - 1))
                    act.wait_ge(L1.sem, L1.at("norm", f))
                    nc.scalar.activation(hl1[:, :, 0, :], t1[:, :, :], ACT.Copy).then_inc(L1.sem, 1)

            steps(act, step)

        @block.vector
        def _(dve):
            V = nc.vector
            V.memset(minus_half[:, :], -0.5).then_inc(s_fill, 1)
            V.memset(xT[:, :], 0.0).then_inc(s_fill, 1)
            V.memset(v1[:, :, :, :], 1.0).then_inc(s_fill, 1)
            V.memset(kvn[:, :, :], 0.0).then_inc(s_fill, 1)
            V.memset(rh[RH:RH + 1, :, :], 1.0).then_inc(s_fill, 1)
            V.memset(ones2[:, :], 1.0).then_inc(s_fill, 1)
            dve.wait_ge(s_fill, 6)
            V.memset(kvn[0:C, :, C:C + 1], 1.0).then_inc(s_fill, 1)
            V.memset(kvn[C:2 * C, :, C + 1:C + 2], 1.0).then_inc(s_fill, 1)
            dve.wait_ge(s_w, 16 * len(weight_loads))
            V.tensor_copy(ident16[:, :], ident)
            V.tensor_copy(pick[:, :, :], pick_in[:, :, :])
            V.tensor_scalar(negative[:, 0:1], gamma, -1.0, None, ALU.mult)
            V.tensor_scalar(negative[:, 1:2], alpha, -1.0, None, ALU.mult)
            V.tensor_copy(b3_hi[:, :], b3[:, :]).then_inc(s_fill, 1)
            dve.wait_ge(s_set, SET.at("vw", 0))
            V.tensor_copy(stack[:, V0:V0 + C], bs[:, 0:C])
            V.tensor_copy(kv_row[:, 1, :], bx[0:1, 0:C]).then_inc(s_set, 1)
            dve.wait_ge(s_set, SET.at("bq", 0))
            V.tensor_copy(bqc[:, :], bs[:, 0:1]).then_inc(s_set, 1)
            V.tensor_reduce(row_mean[:, 0:1], stack[:, Q0:Q0 + C], AX, ALU.add, negate=True)
            V.tensor_reduce(row_mean[:, 1:2], stack[:, K0:K0 + C], AX, ALU.add, negate=True)
            V.tensor_reduce(row_mean[0:1, 2:3], kv_row[:, 0, :], AX, ALU.add, negate=True
                            ).then_inc(s_set, 1)
            dve.wait_ge(s_set, SET.at("mean", 0))
            V.tensor_scalar(row_mean[:, 0:2], row_mean[:, 0:2], 1.0 / C, None, ALU.mult)
            V.tensor_scalar(row_mean[0:1, 2:3], row_mean[0:1, 2:3], 1.0 / C, None, ALU.mult
                            ).then_inc(s_set, 1)
            dve.wait_ge(s_set, SET.at("scaled", 0))
            V.tensor_scalar(stack[:, Q0 + C:Q0 + 2 * C], stack[:, Q0:Q0 + C], row_mean[:, 0:1], None,
                            ALU.add)
            V.tensor_scalar(stack[:, K0:K0 + C], stack[:, K0:K0 + C], row_mean[:, 1:2], None, ALU.add)
            V.tensor_scalar(kv_row[:, 0, :], kv_row[:, 0, :], row_mean[0:1, 2:3], None, ALU.add
                            ).then_inc(s_set, 1)
            dve.wait_ge(s_set, SET.at("centred", 0))
            V.tensor_copy(stack[:, Q0:Q0 + C], stack[:, Q0 + C:Q0 + 2 * C])
            for j in range(NT):
                i = V.tensor_copy(kv_bias[0:1, j, :], kv_row[:, :, :].rearrange("p a c -> p (a c)"))
            i.then_inc(s_set, 1)
            dve.wait_ge(s_set, SET.at("bias", 0))
            V.tensor_copy(stack_hi[:, :], stack[:, :])
            for j in range(NT):
                i = V.tensor_tensor(kv_lo[:, j, :], kv_row[:, :, :].rearrange("p a c -> p (a c)"),
                                    kv_bias[0:1, j, :], ALU.subtract)
            i.then_inc(s_set, 1)
            dve.wait_ge(s_set, SET.at("hilo", 0))
            V.tensor_tensor(b3_lo[:, :], b3[:, :], b3_hi[:, :], ALU.subtract)
            V.tensor_tensor(stack_lo[:, :], stack[:, :], stack_hi[:, :], ALU.subtract
                            ).then_inc(s_set, 1)
            dve.wait_ge(s_fill, 9)

            def per_token(col, n=C):
                return col.unsqueeze(2).to_broadcast([TP, G, n])

            def tap(f, k):
                dve.wait_ge(BN.sem, BN.at(f"tap{k - 1}", f))
                V.scalar_tensor_tensor(out=y[:, :], in0=xT[:, k:k + 2 * T:2],
                                       scalar=conv_w[:, k:k + 1], in1=y[:, :],
                                       op0=ALU.mult, op1=ALU.add).then_inc(BN.sem, 1)

            def gated(n, i):
                j, b = i // 2, i % 2
                if i == 0:
                    if worked(n - 1):
                        dve.wait_ge(EO.sem, EO.at("product1", n - 1))
                dve.wait_ge(E2A.sem, E2A.at(i + 1, n))
                dve.wait_ge(GP.sem, GP.at(i + 1, n))
                V.tensor_tensor(e2g[:, j, b * NT:(b + 1) * NT, :], e2[:, j, b * NT:(b + 1) * NT, :],
                                bk[i % 2][:, 0:T].rearrange("p (j t) -> p j t", j=NT),
                                ALU.mult).then_inc(GA.sem, 1)

            ranks = rank[0:TP, :].unsqueeze(1).to_broadcast([TP, G, E])
            logits = bs[0:TP, 0:G * E].rearrange("p (g e) -> p g e", e=E)

            def largest(m):
                dve.wait_ge(RT.sem, RT.at("logits", m))
                V.tensor_reduce(rs[:, 0, :], logits, AX, ALU.max).then_inc(RT.sem, 1)

            def shift(m):
                dve.wait_ge(RT.sem, RT.at("max", m))
                V.tensor_tensor(rt[:, 0, :, :], logits, per_token(rs[:, 0, :], E), ALU.subtract
                                ).then_inc(RT.sem, 1)

            def total(m):
                dve.wait_ge(RT.sem, RT.at("exp", m))
                V.tensor_reduce(rs[:, 1, :], rt[:, 1, :, :], AX, ALU.add).then_inc(RT.sem, 1)

            def over_total(m):
                dve.wait_ge(RT.sem, RT.at("sum", m))
                V.reciprocal(rs[:, 4, :], rs[:, 1, :]).then_inc(RT.sem, 1)

            def marked(m, k):
                if k == 2:
                    dve.wait_ge(RT.sem, RT.at("gap0", m))
                V.scalar_tensor_tensor(out=rt[:, 3, :, :], in0=rt[:, 0 if k == 1 else 2, :, :],
                                       scalar=0.0, in1=ranks, op0=ALU.is_ge, op1=ALU.mult
                                       ).then_inc(RT.sem, 1)

            def first_of(m, k):
                dve.wait_ge(RT.sem, RT.at(f"marked{k}", m))
                V.tensor_reduce(rs[:, 3, :], rt[:, 3, :, :], AX, ALU.max).then_inc(RT.sem, 1)

            def one_hot(m, k):
                dve.wait_ge(RT.sem, RT.at(f"first{k}", m))
                V.tensor_tensor(rt[:, 3 + k, :, :], rt[:, 3, :, :], per_token(rs[:, 3, :], E),
                                ALU.is_equal).then_inc(RT.sem, 1)

            def rest(m):
                dve.wait_ge(RT.sem, RT.at("one1", m))
                V.scalar_tensor_tensor(out=rt[:, 6, :, :], in0=rt[:, 4, :, :], scalar=-1e30,
                                       in1=rt[:, 0, :, :], op0=ALU.mult, op1=ALU.add
                                       ).then_inc(RT.sem, 1)

            def second(m):
                dve.wait_ge(RT.sem, RT.at("rest", m))
                V.tensor_reduce(rs[:, 7, :], rt[:, 6, :, :], AX, ALU.max).then_inc(RT.sem, 1)

            def below_second(m):
                dve.wait_ge(RT.sem, RT.at("e2", m))
                V.tensor_tensor(rt[:, 2, :, :], rt[:, 6, :, :], per_token(rs[:, 7, :], E),
                                ALU.subtract).then_inc(RT.sem, 1)

            def difference(m):
                dve.wait_ge(RT.sem, RT.at("one2", m))
                V.tensor_tensor(rt[:, 7, :, :], rt[:, 4, :, :], rt[:, 5, :, :], ALU.subtract
                                ).then_inc(RT.sem, 1)
                V.scalar_tensor_tensor(out=rs[:, 5, :], in0=rs[:, 6, :], scalar=-1.0,
                                       in1=rs[:, 4, :], op0=ALU.add, op1=ALU.mult
                                       ).then_inc(RT.sem, 1)

            def softmax_of_two(m):
                dve.wait_ge(RT.sem, RT.at("egap", m))
                V.tensor_scalar(rs[:, 8, :], rs[:, 2, :], 1.0, None, ALU.add).then_inc(RT.sem, 1)

            def weight1(m):
                dve.wait_ge(RT.sem, RT.at("egap1", m))
                V.reciprocal(rs[:, 9, :], rs[:, 8, :]).then_inc(RT.sem, 1)

            def part(m):
                dve.wait_ge(RT.sem, RT.at("w1", m))
                V.tensor_tensor(rt[:, 7, :, :], rt[:, 7, :, :], per_token(rs[:, 9, :], E),
                                ALU.mult).then_inc(RT.sem, 1)

            def gates(m):
                dve.wait_ge(RT.sem, RT.at("part", m))
                V.tensor_tensor(rt[:, 8, :, :], rt[:, 7, :, :], rt[:, 5, :, :], ALU.add
                                ).then_inc(RT.sem, 1)

            def gates_high(m):
                dve.wait_ge(RT.sem, RT.at("gates", m))
                V.tensor_copy(gate[:, :, 0, :], rt[:, 8, :, :]).then_inc(RT.sem, 1)

            def gates_low(m):
                dve.wait_ge(RT.sem, RT.at("high", m))
                V.tensor_tensor(gate[:, :, 1, :], rt[:, 8, :, :], gate[:, :, 0, :],
                                ALU.subtract).then_inc(RT.sem, 1)

            def step(s, slot, at_work):
                F, A, B_, M, N = at_work
                f, a, b, m, n = s, s - 1, s - 2, s - 3, s - 4
                t2p = bt[0:TP, 0:G * (C + 2)].rearrange("p (g c) -> p g c", g=G)
                kv = bs[:, 0:2 * (C + 1)].rearrange("p (b c) -> p b c", b=2)
                if M:
                    if worked(m - 1):
                        dve.wait_ge(E1P.sem, E1P.at(2 * J, m - 1))
                    dve.wait_ge(L2.sem, L2.at("turn", m))
                    V.tensor_copy(l2[:, :, :], bl[:, 0:G * TE].rearrange(
                        "p (g t) -> p g t", g=G)[:, :, 0:TP]).then_inc(L2.sem, 1)
                if F:
                    tap(f, 1)
                if B_:
                    dve.wait_ge(AT.sem, AT.at("t2", b))
                    V.tensor_scalar(at[:, 0, :], t2p[:, :, C], EPS_DIV, None, ALU.add
                                    ).then_inc(AT.sem, 1)
                    dve.wait_ge(AT.sem, AT.at("eps", b))
                    V.reciprocal(at[:, 1, :], at[:, 0, :]).then_inc(AT.sem, 1)
                if F:
                    tap(f, 2)
                if B_:
                    dve.wait_ge(AT.sem, AT.at("recip", b))
                    V.tensor_tensor(at[:, 2, :], t2p[:, :, C + 1], at[:, 1, :], ALU.mult
                                    ).then_inc(AT.sem, 1)
                    dve.wait_ge(AT.sem, AT.at("n1", b))
                    V.tensor_tensor(at[:, 3, :], at[:, 2, :], at[:, 1, :], ALU.mult
                                    ).then_inc(AT.sem, 1)
                    dve.wait_ge(AT.sem, AT.at("n2", b))
                    V.tensor_scalar(at[:, 4, :], at[:, 3, :], EPS_NORM ** 2, None, ALU.max
                                    ).then_inc(AT.sem, 1)
                if F:
                    tap(f, 3)
                    tap(f, 4)
                if M:
                    largest(m)
                if F:
                    dve.wait_ge(BN.sem, BN.at("tap4", f))
                    V.bn_stats(stats[:, :], y[:, :]).then_inc(BN.sem, 1)
                if B_:
                    dve.wait_ge(AT.sem, AT.at("rlen", b))
                    V.tensor_tensor(at[:, 6, :], at[:, 5, :], at[:, 1, :], ALU.mult
                                    ).then_inc(AT.sem, 1)
                if M:
                    shift(m)
                if B_:
                    dve.wait_ge(AT.sem, AT.at("scale", b))
                    V.tensor_tensor(att[:, :, :], t2p[:, :, 0:C], per_token(at[:, 6, :]), ALU.mult
                                    ).then_inc(AT.sem, 1)
                if M:
                    total(m)
                if N:
                    gated(n, 0)
                if A:
                    dve.wait_ge(KE.sem, KE.at(3, a))
                    V.tensor_reduce(ks[:, 0, :], k_sq[:, :, :], AX, ALU.add).then_inc(KN.sem, 1)
                if M:
                    over_total(m)
                    marked(m, 1)
                if A:
                    dve.wait_ge(KN.sem, KN.at("sum", a))
                    V.tensor_scalar(ks[:, 1, :], ks[:, 0, :], EPS_DIV, None, ALU.add
                                    ).then_inc(KN.sem, 1)
                if F:
                    dve.wait_ge(BN.sem, BN.at("stats", f))
                    dve.sem_inc(carrier)
                    V.bn_aggr(bn[:, 0:2], stats[:, :]).then_inc(BN.sem, 1)
                if M:
                    first_of(m, 1)
                if A:
                    dve.wait_ge(KN.sem, KN.at("eps", a))
                    V.reciprocal(ks[:, 2, :], ks[:, 1, :]).then_inc(KN.sem, 1)
                if M:
                    one_hot(m, 1)
                if A:
                    dve.wait_ge(KN.sem, KN.at("recip", a))
                    V.tensor_tensor(kk[:, :, 0, :], k_sq[:, :, :], per_token(ks[:, 2, :]),
                                    ALU.mult).then_inc(KN.sem, 1)
                if M:
                    rest(m)
                if F:
                    dve.wait_ge(BN.sem, BN.at("mean", f))
                    V.tensor_tensor(bn[:, 2:3], bn[:, 0:1], bs[:, 0:1], ALU.subtract
                                    ).then_inc(BN.sem, 1)
                if N:
                    gated(n, 1)
                if F:
                    dve.wait_ge(BN.sem, BN.at("dev", f))
                    V.scalar_tensor_tensor(out=bn[:, 3:4], in0=bn[:, 2:3], scalar=bn[:, 2:3],
                                           in1=bn[:, 1:2], op0=ALU.mult, op1=ALU.add
                                           ).then_inc(BN.sem, 1)
                if M:
                    second(m)
                if B_:
                    hT = bx[0:TP, 0:NT * 128].rearrange("p (j b c) -> p b j c", j=NT, b=2)
                    dve.wait_ge(HT.sem, HT.at(1, b))
                    dve.wait_ge(AT.sem, AT.at("plus_v", b))
                    if worked(b - 2):
                        dve.wait_ge(YR.sem, YR.at(1, b - 2))
                    V.tensor_tensor(h2[:, slot, :, :].rearrange("p (b j) c -> p b j c", b=2),
                                    hT, att_v[:, :, :].rearrange("p (b j) c -> p b j c", b=2),
                                    ALU.add).then_inc(AT.sem, 1)
                if F:
                    dve.wait_ge(BN.sem, BN.at("var", f))
                    V.tensor_scalar(bn[:, 4:5], bs[:, 1:2], EPS_BATCH, None, ALU.add
                                    ).then_inc(BN.sem, 1)
                if N:
                    gated(n, 2)
                    gated(n, 3)
                if F:
                    dve.wait_ge(BN.sem, BN.at("rstd", f))
                    V.tensor_tensor(bn[:, 6:7], bn[:, 5:6], gamma, ALU.mult).then_inc(BN.sem, 1)
                    V.tensor_tensor(bn[:, 9:10], bn[:, 5:6], negative[:, 0:1], ALU.mult
                                    ).then_inc(BN.sem, 1)
                    dve.wait_ge(BN.sem, BN.at("scale", f))
                    V.tensor_tensor(bn[:, 7:8], bn[:, 6:7], bs[:, 0:1], ALU.mult
                                    ).then_inc(BN.sem, 1)
                if N:
                    gated(n, 4)
                if B_:
                    dve.wait_ge(AT.sem, AT.at("h2", b))
                    for g in range(G):
                        i = V.bn_stats(st2[:, g, :], h2[:, slot, g, :])
                    i.then_inc(L2.sem, 1)
                if M:
                    below_second(m)
                if F:
                    dve.wait_ge(BN.sem, BN.at("shift0", f))
                    V.tensor_tensor(bn[:, 8:9], beta, bn[:, 7:8], ALU.subtract
                                    ).then_inc(BN.sem, 1)
                if B_:
                    dve.wait_ge(L2.sem, L2.at("stats", b))
                    V.tensor_tensor(ln2[:, 0, :], st2[:, :, 1], st2[:, :, 4], ALU.subtract
                                    ).then_inc(L2.sem, 1)
                if F:
                    V.tensor_tensor(bn[:, 10:11], bn[:, 7:8], beta, ALU.subtract
                                    ).then_inc(BN.sem, 1)
                if B_:
                    V.tensor_tensor(ln2[:, 1, :], st2[:, :, 1], st2[:, :, 4], ALU.add
                                    ).then_inc(L2.sem, 1)
                    V.tensor_tensor(ln2[:, 2, :], st2[:, :, 2], st2[:, :, 5], ALU.add
                                    ).then_inc(L2.sem, 1)
                    dve.wait_ge(L2.sem, L2.at("dm", b))
                    V.tensor_tensor(ln2[:, 3, :], ln2[:, 0, :], ln2[:, 0, :], ALU.mult
                                    ).then_inc(L2.sem, 1)
                if A:
                    dve.wait_ge(KN.sem, KN.at("kv", a))
                    V.tensor_scalar(kn[:, 0, :], kv[C:2 * C, :, C], EPS_NORM ** 2, None, ALU.max
                                    ).then_inc(KN.sem, 1)
                if M:
                    marked(m, 2)
                if B_:
                    dve.wait_ge(L2.sem, L2.at("dm2", b))
                    V.scalar_tensor_tensor(out=ln2[:, 4, :], in0=ln2[:, 3, :], scalar=C / 4.0,
                                           in1=ln2[:, 2, :], op0=ALU.mult, op1=ALU.add
                                           ).then_inc(L2.sem, 1)
                if M:
                    first_of(m, 2)
                if B_:
                    V.tensor_scalar(ln2[:, 7, :], ln2[:, 1, :], 0.5, None, ALU.mult
                                    ).then_inc(L2.sem, 1)
                    dve.wait_ge(L2.sem, L2.at("var", b))
                    V.tensor_scalar(ln2[:, 5, :], ln2[:, 4, :], 1.0 / C, EPS_LAYER, ALU.mult,
                                    ALU.add).then_inc(L2.sem, 1)
                if M:
                    one_hot(m, 2)
                if N:
                    gated(n, 5)
                if F:
                    if worked(f - 1):
                        dve.wait_ge(L1.sem, L1.at("centred", f - 1))
                    if worked(f - 1):
                        dve.wait_ge(HB.sem, HB.at(1, f - 1))
                    dve.wait_ge(BN.sem, BN.at("below", f))
                    V.scalar_tensor_tensor(out=h[:, :, :], in0=below[:, :, :],
                                           scalar=negative[:, 1:2], in1=above[:, :, :],
                                           op0=ALU.mult, op1=ALU.add).then_inc(BN.sem, 1)
                if M:
                    difference(m)
                if B_:
                    if worked(b - 1):
                        dve.wait_ge(L2.sem, L2.at("low", b - 1))
                    dve.wait_ge(L2.sem, L2.at("mean", b))
                    V.tensor_tensor(t2[:, :, :], h2[:, slot, :, :], per_token(ln2[:, 7, :]),
                                    ALU.subtract).then_inc(CE.sem, 1)
                if M:
                    softmax_of_two(m)
                if B_:
                    dve.wait_ge(CE.sem, CE.at(1, b))
                    dve.wait_ge(L2.sem, L2.at("rstd", b))
                    V.tensor_tensor(t2[:, :, :], t2[:, :, :], per_token(ln2[:, 6, :]),
                                    ALU.mult).then_inc(L2.sem, 1)
                if M:
                    weight1(m)
                    part(m)
                    gates(m)
                if F:
                    dve.wait_ge(L1.sem, L1.at("square", f))
                    V.tensor_reduce(ln1[:, 0, :].rearrange("p (b j) -> p j b", b=2),
                                    sq1[:, :, :, :], AX, ALU.add).then_inc(L1.sem, 1)
                if M:
                    gates_high(m)
                if F:
                    dve.wait_ge(L1.sem, L1.at("sum", f))
                    V.tensor_scalar(ln1[:, 1, :], ln1[:, 0, :], 1.0 / C, EPS_LAYER, ALU.mult,
                                    ALU.add).then_inc(L1.sem, 1)
                if M:
                    gates_low(m)
                    if worked(m - 2):
                        dve.wait_ge(EO.sem, EO.at("product1", m - 2))
                    dve.wait_ge(RT.sem, RT.at("turn", m))
                    V.tensor_copy(gateT[:, 1 - slot, :, :], bl[0:2 * E, 0:G * TE].rearrange(
                        "p (g t) -> p g t", g=G)[:, :, 0:TP]).then_inc(RT.sem, 1)
                if A:
                    dve.wait_ge(KN.sem, KN.at("rlen", a))
                    if worked(a - 1):
                        dve.wait_ge(AT.sem, AT.at("t2", a - 1))
                    for h_ in range(2):
                        V.tensor_scalar(kvn[0:C, h_, 0:C], kv[0:C, h_, 0:C], kn[:, 1, h_:h_ + 1],
                                        float(T) ** -0.5, ALU.mult, ALU.mult).then_inc(KN.sem, 1)
                if F:
                    if worked(f - 1):
                        dve.wait_ge(L1.sem, L1.at("low", f - 1))
                    dve.wait_ge(L1.sem, L1.at("rstd", f))
                    V.tensor_tensor(
                        t1[:, :, :].rearrange("p (b j) c -> p b j c", b=2),
                        bx[0:TP, 0:NT * 128].rearrange("p (j b c) -> p b j c", j=NT, b=2),
                        ln1[:, 2, :].rearrange("p (b j) -> p b j", b=2).unsqueeze(3)
                        .to_broadcast([TP, 2, NT, C]), ALU.mult).then_inc(L1.sem, 1)

            steps(dve, step)


def kernel(**inputs):
    import numpy as np
    import concourse.bacc as bacc
    from concourse.bass_utils import run_bass_kernel_spmd

    x = inputs["x"]
    B, TIN, C = x.shape
    w = {n.split("_", 2)[2]: np.asarray(a) for n, a in inputs.items() if n != "x"}
    E, _, H = w["expert_w1"].shape
    RH = w["router_w1"].shape[1]
    TAPS = w["w"].shape[0]
    J = E // 2
    blocks = np.kron(np.eye(2), np.ones((C, C))) / C
    pick = np.zeros((2 * E, J, 128))
    for e in range(E):
        for part in range(2):
            pick[e + part * E, e // 2, (e % 2) * C:(e % 2 + 1) * C] = 1.0
    const = {"squares": np.stack([np.eye(128), np.eye(128) - blocks, blocks], 1),
             "rank": np.tile(np.arange(E, 0, -1), (128, 1)), "pick": pick}

    def twice(a):
        return np.concatenate([a, a], 0)

    q, k, v = np.split(w["W_qkv"], 3, 1)
    bq, bk, bv = np.split(w["b_qkv"], 3)
    w1 = w["expert_w1"].transpose(1, 0, 2).reshape(C, E * H)
    columns = [twice(w["w"].reshape(TAPS, C).T)]
    columns += [twice(a[:, None]) for a in (w["b"], w["gamma"], w["beta"], w["alpha"], w["b_out"], bq)]
    columns += [w["expert_b1"].reshape(J, 128).T, w["expert_b2"].reshape(J, 128).T]
    columns += [np.concatenate([w["router_b1"], np.zeros(128 - RH, np.float32)])[:, None]]
    w2 = np.zeros((2, H, J, 2, H), np.float32)
    for a in range(2):
        w2[a, :, :, a, :] = w["expert_w2"][a::2].transpose(1, 0, 2)
    laid = {
        "stack": twice(np.concatenate([q, q, k, v, w1, w["router_w1"]], 1)),
        "head": np.concatenate([v.T, v.T, w["W_out"], bv[:, None]], 1),
        "b_k": bk[None], "b3": twice(w["expert_b3"]),
        "wr2": np.concatenate([w["router_w2"], w["router_b2"][None]], 0),
        "w3": w["expert_w3"].reshape(J, 128, C).transpose(1, 0, 2),
        "w2": w2.reshape(128, J, 128), "cols": np.concatenate(columns, 1),
    }
    nc = bacc.Bacc("TRN2", target_bir_lowering=False, num_devices=1)
    arrays = {}

    def given(name, a):
        a = np.ascontiguousarray(a)
        arrays[name] = a
        return nc.dram_tensor(name, a.shape, mybir.dt.from_np(a.dtype), kind="ExternalInput").ap()

    xs = given("x_dram", x)
    ws = {n: given(f"{n}_dram", a) for n, a in laid.items()}
    cs = {n: given(f"{n}_const", a.astype(np.float32)) for n, a in const.items()}
    out = nc.dram_tensor("out_dram", (B, TIN // 2, C), F32, kind="ExternalOutput").ap()
    audio_tower(nc, xs, ws, cs, out, E, H, RH, TAPS)
    r = run_bass_kernel_spmd(nc, [arrays], core_ids=[0])
    return r.results[0]["out_dram"]
```

```python
from contextlib import ExitStack

import concourse.bass as bass
from concourse import mybir

F32 = mybir.dt.float32
F16 = mybir.dt.float16
ALU = mybir.AluOpType
ACT = mybir.ActivationFunctionType
AX = mybir.AxisListType.X

EPS_BATCH = 1e-3
EPS_LAYER = 1e-5
EPS_DIV = 1e-7
EPS_NORM = 1e-12


class Chain:

    def __init__(self, sem, steps):
        self.sem = sem
        self.steps = {name: n + 1 for n, name in enumerate(steps.split())}

    def at(self, step, pair):
        return len(self.steps) * pair + self.steps[step]


class Count:

    def __init__(self, sem, per):
        self.sem, self.per = sem, per

    def at(self, n, pair):
        return self.per * pair + n


def audio_tower(nc, x, w, const, out, E, H, RH, TAPS):
    B, TIN, C = x.shape
    T = out.shape[1]
    PAIRS = B // 2
    P = 2 * C
    NT = 3
    TP = T // NT
    G = 2 * NT
    J = E // 2
    TE = TP + TP % 2
    NX = TIN // TP
    assert P == 128 and C == H and T == NT * TP and TIN == 2 * T and TAPS == 5 and B % 4 == 0

    Q0, K0, V0, E0, R0 = 0, P, P + C, P + 2 * C, P + 2 * C + E * H
    WCOLS = R0 + RH

    with ExitStack() as ctx:
        def sb(name, shape, dt=F32):
            return ctx.enter_context(nc.sbuf_tensor(name, shape, dt))

        def bank(name, dt=F32):
            return ctx.enter_context(nc.psum_tensor(name, [128, 512 if dt == F32 else 1024], dt))

        def sem(name):
            return ctx.enter_context(nc.semaphore(name))

        const_in = sb("const_in", [128, 3, 128])
        ident, centre, average = (const_in[:, i, :] for i in range(3))
        ident16 = sb("ident16", [128, 128], F16)
        pick_in = sb("pick_in", [4 * E, J, 128])
        pick = sb("pick", [4 * E, J, 128], F16)
        rank_in = sb("rank_in", [128, E + 2])
        rank = rank_in[:, 0:E]
        minus_half = sb("minus_half", [128, G])
        stack = sb("stack", [128, WCOLS])
        stack_hi = sb("stack_hi", [128, WCOLS], F16)
        stack_lo = sb("stack_lo", [128, WCOLS], F16)
        head = sb("head", [C, 3 * C + 1])
        wvT, wout, bv = head[:, 0:2 * C], head[:, 2 * C:3 * C], head[:, 3 * C:]
        row_mean = sb("row_mean", [128, 4])
        bqc = sb("bqc", [128, 1])
        kv_row = sb("kv_row", [1, 2, C])
        kv_lo = sb("kv_lo", [1, NT, 2 * C], F16)
        kv_bias = sb("kv_bias", [2, NT, 2 * C], F16)
        ones2 = sb("ones2", [2, TP], F16)
        w2 = sb("w2", [128, J, 128])
        w3 = sb("w3", [128, J, C])
        b3 = sb("b3", [4 * E, C])
        b3_hi = sb("b3_hi", [4 * E, C], F16)
        b3_kept = sb("b3_kept", [4 * E, C])
        b3_parts = sb("b3_parts", [4 * E, C], F16)
        wr2 = sb("wr2", [RH + 1, E])
        cols = sb("cols", [128, TAPS + 6 + 2 * J + 1])
        conv_w = cols[:, 0:TAPS]
        conv_b, gamma, beta, alpha, b_out, bq = (cols[:, TAPS + i:TAPS + i + 1] for i in range(6))
        b1 = cols[:, TAPS + 6:TAPS + 6 + J]
        b2 = cols[:, TAPS + 6 + J:TAPS + 6 + 2 * J]
        br1 = cols[0:RH, TAPS + 6 + 2 * J:]
        negative = sb("negative", [128, 2])

        x_in = sb("x_in", [TP, 2, NX, 2, C])
        xT = sb("xT", [128, TIN + 4])
        y = sb("y", [128, T])
        stats = sb("stats", [128, 6])
        bn = sb("bn", [128, 12])
        above = sb("above", [128, NT, TP])
        below = sb("below", [128, NT, TP])
        h = sb("h", [128, NT, TP])
        hb = sb("hb", [128, 2, NT, TP])
        sq1 = sb("sq1", [TP, NT, 2, C])
        ln1 = sb("ln1", [TP, 3, G])
        hc = sb("hc", [TP, NT, 2, C])
        t1 = sb("t1", [TP, G, C])
        hl1 = sb("hl1", [TP, G, 2, C], F16)
        l1 = sb("l1", [128, G, TP], F16)
        k_sq = sb("k_sq", [TP, G, C])
        ks = sb("ks", [TP, 3, G])
        kk = sb("kk", [TP, G, 2, C])
        v1 = sb("v1", [TP, 2, G, C + 1])
        q2 = sb("q2", [128, G, TP])
        kn = sb("kn", [C, 3, 2])
        kvn = sb("kvn", [128, 2, C + 2])
        at = sb("at", [TP, 8, G])
        att = sb("att", [TP, G, C])
        att_v = sb("att_v", [TP, G, C])
        h2 = sb("h2", [TP, 2, G, C])
        st2 = sb("st2", [TP, G, 6])
        ln2 = sb("ln2", [TP, 8, G])
        t2 = sb("t2", [TP, G, C])
        hl2 = sb("hl2", [TP, G, 2, C], F16)
        l2 = sb("l2", [128, G, TP], F16)
        rh = sb("rh", [RH + 1, G, TP])
        rt = sb("rt", [TP, 9, G, E])
        rs = sb("rs", [TP, 10, G])
        gate = sb("gate", [TP, G, 2, 2, E], F16)
        gateT = sb("gateT", [4 * E, 2, G, TP], F16)
        e1 = sb("e1", [128, J, G, TP])
        e2 = sb("e2", [128, J, G, TP])
        e2g = sb("e2g", [128, J, G, TP])
        e_out = sb("e_out", [TP, G, C])
        y_out = sb("y_out", [TP, 2, G, C])

        bx = bank("bx")
        bk = [bank(f"bk{b}") for b in range(2)]
        bt = bank("bt")
        bl = bank("bl", F16)
        bs = bank("bs")
        bh = [bank(f"bh{i}") for i in range(2)]

        s_c = sem("columns_in")
        s_w = sem("weights_in")
        s_b = sem("low_bias_moved")
        SET = Chain(sem("setup"), "vw vwc bq bqc mean scaled centred bias low_bias high low")
        HALF = Chain(sem("halved"), "kept high low")
        s_fill = sem("filled")
        carrier = sem("carrier")
        x_ready = [sem(f"x_ready{i}") for i in range(2)]
        stored = [sem(f"stored{i}") for i in range(2)]

        XT = Chain(sem("x_turned"), "turn0 copy0 turn1 copy1")
        BN = Chain(sem("front"), "tap0 tap1 tap2 tap3 tap4 stats aggr mean dev var_c var var_eps"
                   " rstd scale nscale shift0 shift nshift above below prelu")
        HB = Count(sem("h_biased"), 1)
        L1 = Chain(sem("layer_norm_1"), "centred square moved sum var rstd norm high low turn copy")
        KP = Count(sem("kv_product"), 2)
        KE = Count(sem("kv_taken"), 4)
        KN = Chain(sem("k_normed"), "sum eps recip k2 k4 kv least rlen kvn0 kvn1")
        QC = Chain(sem("q_squared"), "q0 sq0 q1 sq1 q4")
        HT = Count(sem("h_turned"), 1)
        AT = Chain(sem("attention"), "t2 eps recip n1 n2 least rlen scale scaled plus_v h2")
        L2 = Chain(sem("layer_norm_2"), "stats dm sm m2 dm2 var mean var_eps rstd norm"
                   " high low turn copy")
        CE = Count(sem("centred_2"), 1)
        RP = Count(sem("router_product"), 2)
        RA = Count(sem("router_relu"), 2)
        RT = Chain(sem("routing"), "logits max shifted exp sum recip marked1 first1 one1 rest max2"
                   " e2 gap0 marked2 first2 one2 diff gap egap egap1 w1 part gates high low turn"
                   " copy")
        E1P, E1A = Count(sem("expert1_product"), 2 * J), Count(sem("expert1_relu"), 2 * J)
        E2P, E2A = Count(sem("expert2_product"), 2 * J), Count(sem("expert2_relu"), 2 * J)
        GP, GA = Count(sem("gates_spread"), 2 * J), Count(sem("gated"), 2 * J)
        EO = Chain(sem("experts_out"), "product0 product1 copy")
        YS = Count(sem("residual_added"), 1)
        YR = Count(sem("residual_copied"), 1)

        weight_loads = [
            (stack[:, :], w["stack"]), (head[:, :], w["head"]), (kv_row[:, 0, :], w["b_k"]),
            (pick_in[:, :, :], const["pick"]), (b3[:, :], w["b3"]), (rank_in[:, :], const["rank"]),
            (wr2[:, :], w["wr2"]), (w2[:, :, :], w["w2"]), (w3[:, :, :], w["w3"]),
        ]

        block = ctx.enter_context(nc.Block())

        def loaded(pair, slot):
            return 16 * (pair - slot) + 32

        def steps(eng, run):
            def peeled(s):
                run(s, s % 2, [s == 0] + [0 <= s - stage < PAIRS for stage in range(5)])

            first = 6
            for s in range(first):
                peeled(s)
            with eng.Fori(first // 2, PAIRS // 2) as half:
                for parity in range(2):
                    run(2 * half + parity, parity, [False] + [True] * 5)
            for s in range(PAIRS, PAIRS + 4):
                peeled(s)

        def worked(pair):
            return not isinstance(pair, int) or 0 <= pair < PAIRS

        @block.sync
        def _(sp):
            sp.dma_start(const_in[:, :, :], const["squares"]).then_inc(s_c, 16)

            def load(pair, slot):
                for b in range(2):
                    sp.dma_start(x_in[:, slot, :, b, :],
                                 x[bass.ds(2 * pair + b, 1)].rearrange("o (p j) c -> p (o j) c", j=NX)
                                 ).then_inc(x_ready[slot], 16)

            load(0, 0)
            for dst, src in weight_loads[0::2]:
                sp.dma_start(dst, src).then_inc(s_w, 16)
            load(1, 1)
            sp.wait_ge(SET.sem, SET.at("low_bias", 0))
            sp.dma_start(kv_bias[1:2, :, :], kv_lo[:, :, :]).then_inc(s_b, 16)

            def step(s, slot):
                if worked(s):
                    if worked(s - 2):
                        sp.wait_ge(XT.sem, XT.at("turn1", s - 2))
                    load(s, slot)
                if worked(s - 5):
                    sp.wait_ge(YS.sem, YS.at(1, s - 5))
                    for b in range(2):
                        sp.dma_start(
                            out[bass.ds(2 * (s - 5) + b, 1)].rearrange("o (p j) c -> p (o j) c", j=NT),
                            y_out[:, 1 - slot, b * NT:(b + 1) * NT, :]).then_inc(stored[1 - slot], 16)

            for s in range(2, 6):
                step(s, s % 2)
            with sp.Fori(3, PAIRS // 2) as half:
                for parity in range(2):
                    step(2 * half + parity, parity)
            for s in range(PAIRS, PAIRS + 5):
                step(s, s % 2)
            for slot in range(2):
                sp.wait_ge(stored[slot], 16 * PAIRS)

        @block.gpsimd
        def _(pool):
            pool.wait_ge(s_fill, 8)

            def step(s, slot, at_work):
                S, F, A, B_, M, N = at_work
                f, a, b, m, n = s, s - 1, s - 2, s - 3, s - 4
                if M:
                    pool.wait_ge(L2.sem, L2.at("high", m))
                    nc.gpsimd.tensor_tensor(hl2[:, :, 1, :], t2[:, :, :], hl2[:, :, 0, :],
                                            ALU.subtract).then_inc(L2.sem, 1)
                if A:
                    pool.wait_ge(L1.sem, L1.at("high", a))
                    nc.gpsimd.tensor_tensor(hl1[:, :, 1, :], t1[:, :, :], hl1[:, :, 0, :],
                                            ALU.subtract).then_inc(L1.sem, 1)
                if B_:
                    pool.wait_ge(AT.sem, AT.at("least", b))
                    nc.gpsimd.tensor_tensor(at[:, 5, :], at[:, 4, :], minus_half[0:TP, :],
                                            ALU.pow).then_inc(AT.sem, 1)
                    pool.wait_ge(AT.sem, AT.at("scaled", b))
                    nc.gpsimd.tensor_tensor(att_v[:, :, :], att[:, :, :], v1[:, slot, :, 0:C],
                                            ALU.add).then_inc(AT.sem, 1)
                if M:
                    pool.wait_ge(AT.sem, AT.at("h2", m))
                    if worked(m - 2):
                        pool.wait_ge(stored[1 - slot], 16 * (m - 2 - (1 - slot)) + 32)
                    pool.sem_inc(carrier)
                    nc.gpsimd.tensor_copy(y_out[:, 1 - slot, :, :], h2[:, 1 - slot, :, :]
                                          ).then_inc(YR.sem, 1)
                if A:
                    pool.wait_ge(KN.sem, KN.at("k2", a))
                    nc.gpsimd.tensor_tensor(kk[:, :, 1, :], kk[:, :, 0, :], kk[:, :, 0, :],
                                            ALU.mult).then_inc(KN.sem, 1)
                if F:
                    pool.wait_ge(BN.sem, BN.at("var_eps", f))
                    nc.gpsimd.tensor_tensor(bn[:, 5:6], bn[:, 4:5], minus_half[:, 0:1],
                                            ALU.pow).then_inc(BN.sem, 1)
                if A:
                    if F:
                        pool.wait_ge(BN.sem, BN.at("rstd", f))
                    else:
                        pool.wait_ge(KN.sem, KN.at("k4", a))
                    pool.wait_ge(QC.sem, QC.at("sq1", a))
                    nc.gpsimd.tensor_tensor(q2[C:2 * C, :, :], q2[C:2 * C, :, :], q2[C:2 * C, :, :],
                                            ALU.mult).then_inc(QC.sem, 1)
                if S:
                    pool.wait_ge(SET.sem, SET.at("high", 0))
                    nc.gpsimd.tensor_tensor(stack_lo[:, :], stack[:, :], stack_hi[:, :],
                                            ALU.subtract).then_inc(SET.sem, 1)
                if A:
                    pool.wait_ge(QC.sem, QC.at("q4", a))
                    pool.wait_ge(KN.sem, KN.at("least", a))
                    nc.gpsimd.tensor_tensor(kn[:, 1, :], kn[:, 0, :], minus_half[0:C, 0:2],
                                            ALU.pow).then_inc(KN.sem, 1)
                if B_:
                    if A:
                        pool.wait_ge(KN.sem, KN.at("rlen", a))
                    pool.wait_ge(L2.sem, L2.at("var_eps", b))
                    nc.gpsimd.tensor_tensor(ln2[:, 6, :], ln2[:, 5, :], minus_half[0:TP, :],
                                            ALU.pow).then_inc(L2.sem, 1)
                if F:
                    if A:
                        pool.wait_ge(KN.sem, KN.at("rlen", a))
                    pool.wait_ge(L1.sem, L1.at("var", f))
                    nc.gpsimd.tensor_tensor(ln1[:, 2, :], ln1[:, 1, :], minus_half[0:TP, :],
                                            ALU.pow).then_inc(L1.sem, 1)
                if N:
                    if A:
                        pool.wait_ge(KN.sem, KN.at("rlen", a))
                    pool.wait_ge(YR.sem, YR.at(1, n))
                    pool.wait_ge(EO.sem, EO.at("copy", n))
                    nc.gpsimd.tensor_tensor(y_out[:, slot, :, :], y_out[:, slot, :, :],
                                            e_out[:, :, :], ALU.add).then_inc(YS.sem, 1)

            steps(pool, step)

        @block.tensor
        def _(pe):
            pe.wait_ge(s_c, 32)

            def turn_split(bank_, hl, chain):
                for g in range(G):
                    i = nc.tensor.transpose(bank_[:, g * TE:g * TE + TP],
                                            hl[:, g, :, :].rearrange("p a c -> p (a c)"),
                                            ident16[0:TP, 0:TP])
                i.then_inc(chain.sem, 1)

            def split_product(dst, l, col, n, b):
                rhs = l[:, b * NT:(b + 1) * NT, :]
                nc.tensor.matmul(dst, stack_hi[:, col:col + n], rhs, start=True, stop=False)
                return nc.tensor.matmul(dst, stack_lo[:, col:col + n], rhs, start=False, stop=True)

            def expert1(m, i, N):
                j, b = i // 2, i % 2
                if i == 0:
                    pe.wait_ge(L2.sem, L2.at("copy", m))
                if i >= 2:
                    pe.wait_ge(E1A.sem, E1A.at(i - 1, m))
                elif N:
                    if worked(m - 1):
                        pe.wait_ge(E2A.sem, E2A.at(2 * J - 1 + i, m - 1))
                split_product(bh[i % 2][:, 0:T], l2, E0 + j * 128, 128, b).then_inc(E1P.sem, 1)

            def expert2(n, i):
                j, b = i // 2, i % 2
                if i < 2:
                    pe.wait_ge(E1A.sem, E1A.at(2 * J - 1 + i, n))
                else:
                    pe.wait_ge(E2A.sem, E2A.at(i - 1, n))
                nc.tensor.matmul(bh[i % 2][:, 0:T], w2[:, j, :], e1[:, j, b * NT:(b + 1) * NT, :],
                                 start=True, stop=True).then_inc(E2P.sem, 1)

            def spread(n, slot, A, M, i):
                j, b = i // 2, i % 2
                if i >= 2:
                    pe.wait_ge(GA.sem, GA.at(i - 1, n))
                elif A:
                    pe.wait_ge(KE.sem, KE.at(2 * i + 2, n + 3))
                elif M:
                    pe.wait_ge(RA.sem, RA.at(i + 1, n + 1))
                elif worked(n - 1):
                    pe.wait_ge(GA.sem, GA.at(2 * J - 1 + i, n - 1))
                if i == 0:
                    pe.wait_ge(RT.sem, RT.at("copy", n))
                nc.tensor.matmul(bk[i % 2][:, 0:T], pick[:, j, :],
                                 gateT[:, slot, b * NT:(b + 1) * NT, :],
                                 start=True, stop=True).then_inc(GP.sem, 1)

            def turn_x(f, slot, half):
                for j in range(NX // 2):
                    i = nc.tensor.transpose(
                        bx[:, j * TP:(j + 1) * TP],
                        x_in[:, slot, half * NX // 2 + j, :, :].rearrange("p b c -> p (b c)"),
                        ident[0:TP, 0:TP])
                i.then_inc(XT.sem, 1)

            def router_hidden(m, h_):
                if h_ == 0:
                    pe.wait_ge(L2.sem, L2.at("copy", m))
                if worked(m - 2):
                    pe.wait_ge(GA.sem, GA.at(2 * J - 1 + h_, m - 2))
                else:
                    pe.wait_ge(KE.sem, KE.at(2 * h_ + 2, m + 1))
                split_product(bk[h_][0:RH, 0:T], l2, R0, RH, h_).then_inc(RP.sem, 1)

            def keys_values(a, M, h_):
                if h_ == 0:
                    pe.wait_ge(L1.sem, L1.at("copy", a))
                if M:
                    pe.wait_ge(RA.sem, RA.at(h_ + 1, a - 2))
                elif worked(a - 1):
                    pe.wait_ge(KE.sem, KE.at(2 * h_ + 2, a - 1))
                nc.tensor.matmul(bk[h_][0:TP, 0:NT * 2 * C], ones2[:, :], kv_bias[:, :, :],
                                 start=True, stop=False, skip_group_check=True)
                for j in range(NT):
                    dst = bk[h_][0:TP, j * 2 * C:(j + 1) * 2 * C]
                    nc.tensor.matmul(dst, l1[:, h_ * NT + j, :], stack_hi[:, K0:E0],
                                     start=False, stop=False, skip_group_check=True)
                    i = nc.tensor.matmul(dst, l1[:, h_ * NT + j, :], stack_lo[:, K0:E0],
                                         start=False, stop=j == NT - 1, skip_group_check=True)
                i.then_inc(KP.sem, 1)

            def queries(a, F, h_):
                if h_ == 0:
                    pe.wait_ge(L1.sem, L1.at("copy", a))
                if h_ == 1:
                    pe.wait_ge(QC.sem, QC.at("sq0", a))
                elif F:
                    pe.wait_ge(XT.sem, XT.at("copy1", a + 1))
                else:
                    pe.wait_ge(L1.sem, L1.at("moved", a))
                split_product(bx[:, 0:T], l1, Q0, 128, h_).then_inc(QC.sem, 1)

            def third_layers(n, slot, B_, half):
                pe.wait_ge(GA.sem, GA.at(2 * J - 1 + half, n))
                if half == 0:
                    if B_:
                        pe.wait_ge(AT.sem, AT.at("scaled", n + 2))
                    elif worked(n - 1):
                        pe.wait_ge(EO.sem, EO.at("copy", n - 1))
                for g in range(half * NT, (half + 1) * NT):
                    dst = bt[0:TP, g * C:(g + 1) * C]
                    nc.tensor.matmul(dst, gateT[:, slot, g, :], b3_parts[:, :],
                                     start=True, stop=False)
                    for j in range(J):
                        i = nc.tensor.matmul(dst, e2g[:, j, g, :], w3[:, j, :],
                                             start=False, stop=j == J - 1)
                i.then_inc(EO.sem, 1)

            def step(s, slot, at_work):
                S, F, A, B_, M, N = at_work
                f, a, b, m, n = s, s - 1, s - 2, s - 3, s - 4
                if F:
                    pe.wait_ge(x_ready[slot], loaded(f, slot))
                    if worked(f - 1):
                        pe.wait_ge(L1.sem, L1.at("moved", f - 1))
                    turn_x(f, slot, 0)
                if N:
                    expert2(n, 0)
                    expert2(n, 1)
                    pe.wait_ge(RT.sem, RT.at("low", n))
                    if worked(b):
                        pe.wait_ge(L1.sem, L1.at("copy", b))
                    else:
                        pe.wait_ge(L2.sem, L2.at("copy", n))
                    for g in range(G):
                        i = nc.tensor.transpose(bl[0:4 * E, g * TE:g * TE + TP],
                                                gate[:, g, :, :, :].rearrange("p d a e -> p (d a e)"),
                                                ident16[0:TP, 0:TP])
                    i.then_inc(RT.sem, 1)
                if F:
                    pe.wait_ge(XT.sem, XT.at("copy0", f))
                    turn_x(f, slot, 1)
                if S:
                    pe.wait_ge(s_w, 16 * len(weight_loads))
                    nc.tensor.matmul(bh[0][:, 0:C], wvT, wout, start=True, stop=True)
                    nc.tensor.matmul(bh[1][0:1, 0:C], bv, wout, start=True, stop=True
                                     ).then_inc(SET.sem, 1)
                    pe.wait_ge(SET.sem, SET.at("vwc", 0))
                    nc.tensor.matmul(bt[:, 0:1], centre, bq, start=True, stop=True
                                     ).then_inc(SET.sem, 1)
                if B_:
                    pe.wait_ge(QC.sem, QC.at("q4", b))
                    pe.wait_ge(KN.sem, KN.at("kvn1", b))
                    if worked(n - 1):
                        pe.wait_ge(EO.sem, EO.at("copy", n - 1))
                    elif worked(b - 1):
                        pe.wait_ge(AT.sem, AT.at("scaled", b - 1))
                    for g in range(G):
                        i = nc.tensor.matmul(bt[0:TP, g * (C + 2):(g + 1) * (C + 2)], q2[:, g, :],
                                             kvn[:, g // NT, :], start=True, stop=True)
                    i.then_inc(AT.sem, 1)
                if M:
                    pe.wait_ge(L2.sem, L2.at("low", m))
                    if N:
                        pe.wait_ge(RT.sem, RT.at("copy", n))
                    else:
                        pe.wait_ge(L1.sem, L1.at("copy", b))
                    turn_split(bl, hl2, L2)
                if N:
                    expert2(n, 2)
                if A:
                    pe.wait_ge(L1.sem, L1.at("low", a))
                    if M:
                        pe.wait_ge(L2.sem, L2.at("copy", m))
                    elif worked(a - 1):
                        pe.wait_ge(L1.sem, L1.at("copy", a - 1))
                    turn_split(bl, hl1, L1)
                if M:
                    router_hidden(m, 0)
                    router_hidden(m, 1)
                if N:
                    expert2(n, 3)
                if A:
                    queries(a, F, 0)
                    keys_values(a, M, 0)
                    keys_values(a, M, 1)
                    queries(a, F, 1)
                if N:
                    spread(n, slot, A, M, 0)
                if M:
                    pe.wait_ge(RA.sem, RA.at(2, m))
                    if worked(s - 2):
                        pe.wait_ge(KN.sem, KN.at("kvn1", s - 2))
                    elif worked(m - 1):
                        pe.wait_ge(RT.sem, RT.at("shifted", m - 1))
                    for g in range(G):
                        i = nc.tensor.matmul(bs[0:TP, g * E:(g + 1) * E], rh[:, g, :], wr2[:, :],
                                             start=True, stop=True)
                    i.then_inc(RT.sem, 1)
                if N:
                    spread(n, slot, A, M, 1)
                    expert2(n, 4)
                if F:
                    pe.wait_ge(BN.sem, BN.at("aggr", f))
                    if M:
                        pe.wait_ge(RT.sem, RT.at("shifted", m))
                    if worked(f - 2):
                        pe.wait_ge(KN.sem, KN.at("kvn1", f - 2))
                    nc.tensor.matmul(bs[:, 0:1], average, bn[:, 0:1], start=True, stop=True
                                     ).then_inc(BN.sem, 1)
                if N:
                    spread(n, slot, A, M, 2)
                    expert2(n, 5)
                if B_:
                    pe.wait_ge(HB.sem, HB.at(1, b))
                    if A:
                        pe.wait_ge(QC.sem, QC.at("sq1", a))
                    elif worked(b - 1):
                        pe.wait_ge(AT.sem, AT.at("h2", b - 1))
                    for j in range(NT):
                        i = nc.tensor.transpose(bx[0:TP, j * 128:(j + 1) * 128], hb[:, slot, j, :],
                                                ident)
                    i.then_inc(HT.sem, 1)
                if M:
                    expert1(m, 0, N)
                if F:
                    pe.wait_ge(BN.sem, BN.at("var_c", f))
                    nc.tensor.matmul(bs[:, 1:2], average, bn[:, 3:4], start=True, stop=True
                                     ).then_inc(BN.sem, 1)
                if N:
                    spread(n, slot, A, M, 3)
                if M:
                    expert1(m, 1, N)
                if N:
                    spread(n, slot, A, M, 4)
                if A:
                    pe.wait_ge(KN.sem, KN.at("k4", a))
                    pe.wait_ge(KE.sem, KE.at(4, a))
                    if F:
                        pe.wait_ge(BN.sem, BN.at("var_eps", f))
                    elif M:
                        pe.wait_ge(RT.sem, RT.at("shifted", m))
                    for h_ in range(2):
                        for j in range(NT):
                            g = h_ * NT + j
                            i = nc.tensor.matmul(bs[:, h_ * (C + 1):(h_ + 1) * (C + 1)],
                                                 kk[:, g, :, :], v1[:, 1 - slot, g, :],
                                                 start=j == 0, stop=j == NT - 1)
                    i.then_inc(KN.sem, 1)
                if M:
                    expert1(m, 2, N)
                if N:
                    spread(n, slot, A, M, 5)
                if M:
                    expert1(m, 3, N)
                if N:
                    third_layers(n, slot, B_, 0)
                if F:
                    pe.wait_ge(BN.sem, BN.at("prelu", f))
                    if B_:
                        pe.wait_ge(AT.sem, AT.at("h2", b))
                    elif A:
                        pe.wait_ge(QC.sem, QC.at("sq1", a))
                    for j in range(NT):
                        i = nc.tensor.matmul(bx[0:TP, j * 128:(j + 1) * 128], h[:, j, :],
                                             centre, start=True, stop=True)
                    i.then_inc(L1.sem, 1)
                if M:
                    expert1(m, 4, N)
                    expert1(m, 5, N)
                if N:
                    third_layers(n, slot, B_, 1)
                if S:
                    pe.wait_ge(SET.sem, SET.at("low", 0))
                    pe.wait_ge(HALF.sem, HALF.at("low", 0))
                    pe.wait_ge(s_b, 16)
                    pe.wait_ge(s_fill, 8)

            steps(pe, step)

        @block.scalar
        def _(act):
            act.dma_start(cols[:, :], w["cols"]).then_inc(s_c, 16)
            for dst, src in weight_loads[1::2]:
                act.dma_start(dst, src).then_inc(s_w, 16)
            act.wait_ge(s_fill, 1)
            nc.scalar.activation(ones2[:, :], minus_half[0:2, 0:1].to_broadcast([2, TP]), ACT.Copy,
                                 scale=-2.0).then_inc(s_fill, 1)
            act.wait_ge(s_fill, 8)
            act.wait_ge(s_c, 32)

            def expert_relu(P_, A_, dst, bias, pair, i):
                j, b = i // 2, i % 2
                act.wait_ge(P_.sem, P_.at(i + 1, pair))
                nc.scalar.activation(dst[:, j, b * NT:(b + 1) * NT, :],
                                     bh[i % 2][:, 0:T].rearrange("p (j t) -> p j t", j=NT),
                                     ACT.Relu, bias=bias[:, j:j + 1]).then_inc(A_.sem, 1)

            def relu1(m, i):
                if i == 0:
                    if worked(m - 1):
                        act.wait_ge(E2P.sem, E2P.at(2 * J, m - 1))
                expert_relu(E1P, E1A, e1, b1, m, i)

            def relu2(n, i):
                if i == 0:
                    if worked(n - 1):
                        act.wait_ge(GA.sem, GA.at(2 * J, n - 1))
                expert_relu(E2P, E2A, e2, b2, n, i)

            def copy_x(f, half):
                act.wait_ge(XT.sem, XT.at(f"turn{half}", f))
                if half == 0:
                    if worked(f - 1):
                        act.wait_ge(BN.sem, BN.at("tap4", f - 1))
                dst = xT[:, 1:1 + TIN].rearrange("p (t j) -> p j t", j=NX)
                nc.scalar.activation(dst[:, half * NX // 2:(half + 1) * NX // 2, :],
                                     bx[:, 0:T].rearrange("p (j t) -> p j t", j=NX // 2),
                                     ACT.Copy).then_inc(XT.sem, 1)

            def router_relu(m, h_):
                act.wait_ge(RP.sem, RP.at(h_ + 1, m))
                if h_ == 0:
                    if worked(m - 1):
                        act.wait_ge(RT.sem, RT.at("logits", m - 1))
                nc.scalar.activation(rh[0:RH, h_ * NT:(h_ + 1) * NT, :],
                                     bk[h_][0:RH, 0:T].rearrange("p (j t) -> p j t", j=NT),
                                     ACT.Relu, bias=br1).then_inc(RA.sem, 1)

            def take_kv(a, slot, h_):
                kv = bk[h_][0:TP, 0:NT * 2 * C].rearrange("p (j c) -> p j c", j=NT)
                act.wait_ge(KP.sem, KP.at(h_ + 1, a))
                if h_ == 0:
                    if worked(a - 1):
                        act.wait_ge(KN.sem, KN.at("kv", a - 1))
                    if worked(a - 2):
                        act.wait_ge(AT.sem, AT.at("plus_v", a - 2))
                nc.scalar.activation(k_sq[:, h_ * NT:(h_ + 1) * NT, :], kv[:, :, 0:C],
                                     ACT.Square).then_inc(KE.sem, 1)
                nc.scalar.activation(v1[:, 1 - slot, h_ * NT:(h_ + 1) * NT, 0:C],
                                     kv[:, :, C:2 * C], ACT.Copy).then_inc(KE.sem, 1)

            def square_q(a, h_):
                act.wait_ge(QC.sem, QC.at(f"q{h_}", a))
                if h_ == 0:
                    if worked(a - 1):
                        act.wait_ge(AT.sem, AT.at("t2", a - 1))
                nc.scalar.activation(q2[:, h_ * NT:(h_ + 1) * NT, :],
                                     bx[:, 0:T].rearrange("p (j t) -> p j t", j=NT),
                                     ACT.Square, bias=bqc[:, :]).then_inc(QC.sem, 1)

            def step(s, slot, at_work):
                S, F, A, B_, M, N = at_work
                f, a, b, m, n = s, s - 1, s - 2, s - 3, s - 4
                if F:
                    copy_x(f, 0)
                if M:
                    if worked(m - 1):
                        act.wait_ge(L2.sem, L2.at("turn", m - 1))
                    act.wait_ge(L2.sem, L2.at("norm", m))
                    nc.scalar.activation(hl2[:, :, 0, :], t2[:, :, :], ACT.Copy).then_inc(L2.sem, 1)
                if N:
                    relu2(n, 0)
                if A:
                    if worked(a - 1):
                        act.wait_ge(L1.sem, L1.at("turn", a - 1))
                    act.wait_ge(L1.sem, L1.at("norm", a))
                    nc.scalar.activation(hl1[:, :, 0, :], t1[:, :, :], ACT.Copy).then_inc(L1.sem, 1)
                if F:
                    copy_x(f, 1)
                    act.wait_ge(XT.sem, XT.at("copy1", f))
                    if worked(f - 1):
                        act.wait_ge(BN.sem, BN.at("below", f - 1))
                    nc.scalar.activation(y[:, :], xT[:, 0:2 * T:2], ACT.Identity, bias=conv_b,
                                         scale=conv_w[:, 0:1]).then_inc(BN.sem, 1)
                if N:
                    relu2(n, 1)
                if A:
                    if worked(a - 1):
                        act.wait_ge(QC.sem, QC.at("q1", a - 1))
                    act.wait_ge(L1.sem, L1.at("turn", a))
                    nc.scalar.activation(l1[:, :, :], bl[:, 0:G * TE].rearrange(
                        "p (g t) -> p g t", g=G)[:, :, 0:TP], ACT.Copy).then_inc(L1.sem, 1)
                if M:
                    router_relu(m, 0)
                    router_relu(m, 1)
                if A:
                    square_q(a, 0)
                    take_kv(a, slot, 0)
                    take_kv(a, slot, 1)
                if N:
                    relu2(n, 2)
                    relu2(n, 3)
                if A:
                    square_q(a, 1)
                if M:
                    act.wait_ge(RT.sem, RT.at("shifted", m))
                    nc.scalar.activation(rt[:, 1, :, :], rt[:, 0, :, :], ACT.Exp).then_inc(RT.sem, 1)
                if N:
                    relu2(n, 4)
                if S:
                    act.wait_ge(s_w, 16 * len(weight_loads))
                    nc.scalar.activation(ident16[:, :], ident, ACT.Copy)
                    nc.scalar.activation(pick[:, :, :], pick_in[:, :, :], ACT.Copy)
                    act.wait_ge(HALF.sem, HALF.at("kept", 0))
                    nc.scalar.activation(b3_hi[:, :], b3[:, :], ACT.Copy).then_inc(HALF.sem, 1)
                if N:
                    relu2(n, 5)
                if M:
                    relu1(m, 0)
                    relu1(m, 1)
                if F:
                    by_tile = y[:, :].rearrange("p (t j) -> p j t", j=NT)
                    act.wait_ge(BN.sem, BN.at("nshift", f))
                    nc.scalar.activation(above[:, :, :], by_tile, ACT.Relu, bias=bn[:, 8:9],
                                         scale=bn[:, 6:7]).then_inc(BN.sem, 1)
                if M:
                    act.wait_ge(RT.sem, RT.at("max2", m))
                    nc.scalar.activation(rs[:, 6, :], rs[:, 7, :], ACT.Exp).then_inc(RT.sem, 1)
                if F:
                    nc.scalar.activation(below[:, :, :], by_tile, ACT.Relu, bias=bn[:, 10:11],
                                         scale=bn[:, 9:10]).then_inc(BN.sem, 1)
                if M:
                    relu1(m, 2)
                    relu1(m, 3)
                    act.wait_ge(RT.sem, RT.at("gap", m))
                    nc.scalar.activation(rs[:, 2, :], rs[:, 5, :], ACT.Exp).then_inc(RT.sem, 1)
                if S:
                    act.wait_ge(SET.sem, SET.at("low_bias", 0))
                    nc.scalar.activation(stack_hi[:, :], stack[:, :], ACT.Copy
                                         ).then_inc(SET.sem, 1)
                if F:
                    act.wait_ge(L1.sem, L1.at("centred", f))
                    nc.scalar.activation(sq1[:, :, :, :].rearrange("p j b c -> p (j b c)"),
                                         bx[0:TP, 0:NT * 128], ACT.Square).then_inc(L1.sem, 1)
                    nc.scalar.activation(hc[:, :, :, :].rearrange("p j b c -> p (j b c)"),
                                         bx[0:TP, 0:NT * 128], ACT.Copy).then_inc(L1.sem, 1)
                if M:
                    relu1(m, 4)
                    relu1(m, 5)
                if F:
                    if worked(f - 2):
                        act.wait_ge(HT.sem, HT.at(1, f - 2))
                    act.wait_ge(BN.sem, BN.at("prelu", f))
                    nc.scalar.activation(hb[:, slot, :, :], h[:, :, :], ACT.Identity, bias=b_out
                                         ).then_inc(HB.sem, 1)
                if N:
                    if worked(n - 1):
                        act.wait_ge(YS.sem, YS.at(1, n - 1))
                    act.wait_ge(EO.sem, EO.at("product1", n))
                    nc.scalar.activation(e_out[:, :, :], bt[0:TP, 0:G * C].rearrange(
                        "p (g c) -> p g c", g=G), ACT.Copy).then_inc(EO.sem, 1)

            steps(act, step)

        @block.vector
        def _(dve):
            V = nc.vector
            V.memset(minus_half[:, :], -0.5).then_inc(s_fill, 1)
            V.memset(xT[:, :], 0.0).then_inc(s_fill, 1)
            V.memset(v1[:, :, :, :], 1.0).then_inc(s_fill, 1)
            V.memset(kvn[:, :, :], 0.0).then_inc(s_fill, 1)
            V.memset(rh[RH:RH + 1, :, :], 1.0).then_inc(s_fill, 1)
            dve.wait_ge(s_fill, 6)
            V.memset(kvn[0:C, :, C:C + 1], 1.0).then_inc(s_fill, 1)
            V.memset(kvn[C:2 * C, :, C + 1:C + 2], 1.0).then_inc(s_fill, 1)
            dve.wait_ge(s_fill, 8)
            dve.wait_ge(s_c, 32)
            V.tensor_scalar(negative[:, 0:1], gamma, -1.0, None, ALU.mult)
            V.tensor_scalar(negative[:, 1:2], alpha, -1.0, None, ALU.mult).then_inc(s_fill, 1)
            dve.wait_ge(s_fill, 9)

            def per_token(col, n=C):
                return col.unsqueeze(2).to_broadcast([TP, G, n])

            def tap(f, k):
                dve.wait_ge(BN.sem, BN.at(f"tap{k - 1}", f))
                V.scalar_tensor_tensor(out=y[:, :], in0=xT[:, k:k + 2 * T:2],
                                       scalar=conv_w[:, k:k + 1], in1=y[:, :],
                                       op0=ALU.mult, op1=ALU.add).then_inc(BN.sem, 1)

            def gated(n, i):
                j, b = i // 2, i % 2
                if i == 0:
                    if worked(n - 1):
                        dve.wait_ge(EO.sem, EO.at("product1", n - 1))
                dve.wait_ge(E2A.sem, E2A.at(i + 1, n))
                dve.wait_ge(GP.sem, GP.at(i + 1, n))
                V.tensor_tensor(e2g[:, j, b * NT:(b + 1) * NT, :], e2[:, j, b * NT:(b + 1) * NT, :],
                                bk[i % 2][:, 0:T].rearrange("p (j t) -> p j t", j=NT),
                                ALU.mult).then_inc(GA.sem, 1)

            ranks = rank[0:TP, :].unsqueeze(1).to_broadcast([TP, G, E])
            logits = bs[0:TP, 0:G * E].rearrange("p (g e) -> p g e", e=E)

            def largest(m):
                dve.wait_ge(RT.sem, RT.at("logits", m))
                V.tensor_reduce(rs[:, 0, :], logits, AX, ALU.max).then_inc(RT.sem, 1)

            def shift(m):
                dve.wait_ge(RT.sem, RT.at("max", m))
                V.tensor_tensor(rt[:, 0, :, :], logits, per_token(rs[:, 0, :], E), ALU.subtract
                                ).then_inc(RT.sem, 1)

            def total(m):
                dve.wait_ge(RT.sem, RT.at("exp", m))
                V.tensor_reduce(rs[:, 1, :], rt[:, 1, :, :], AX, ALU.add).then_inc(RT.sem, 1)

            def over_total(m):
                dve.wait_ge(RT.sem, RT.at("sum", m))
                V.reciprocal(rs[:, 4, :], rs[:, 1, :]).then_inc(RT.sem, 1)

            def marked(m, k):
                if k == 2:
                    dve.wait_ge(RT.sem, RT.at("gap0", m))
                V.scalar_tensor_tensor(out=rt[:, 3, :, :], in0=rt[:, 0 if k == 1 else 2, :, :],
                                       scalar=0.0, in1=ranks, op0=ALU.is_ge, op1=ALU.mult
                                       ).then_inc(RT.sem, 1)

            def first_of(m, k):
                dve.wait_ge(RT.sem, RT.at(f"marked{k}", m))
                V.tensor_reduce(rs[:, 3, :], rt[:, 3, :, :], AX, ALU.max).then_inc(RT.sem, 1)

            def one_hot(m, k):
                dve.wait_ge(RT.sem, RT.at(f"first{k}", m))
                V.tensor_tensor(rt[:, 3 + k, :, :], rt[:, 3, :, :], per_token(rs[:, 3, :], E),
                                ALU.is_equal).then_inc(RT.sem, 1)

            def rest(m):
                dve.wait_ge(RT.sem, RT.at("one1", m))
                V.scalar_tensor_tensor(out=rt[:, 6, :, :], in0=rt[:, 4, :, :], scalar=-1e30,
                                       in1=rt[:, 0, :, :], op0=ALU.mult, op1=ALU.add
                                       ).then_inc(RT.sem, 1)

            def second(m):
                dve.wait_ge(RT.sem, RT.at("rest", m))
                V.tensor_reduce(rs[:, 7, :], rt[:, 6, :, :], AX, ALU.max).then_inc(RT.sem, 1)

            def below_second(m):
                dve.wait_ge(RT.sem, RT.at("e2", m))
                V.tensor_tensor(rt[:, 2, :, :], rt[:, 6, :, :], per_token(rs[:, 7, :], E),
                                ALU.subtract).then_inc(RT.sem, 1)

            def difference(m):
                dve.wait_ge(RT.sem, RT.at("one2", m))
                V.tensor_tensor(rt[:, 7, :, :], rt[:, 4, :, :], rt[:, 5, :, :], ALU.subtract
                                ).then_inc(RT.sem, 1)
                V.scalar_tensor_tensor(out=rs[:, 5, :], in0=rs[:, 6, :], scalar=-1.0,
                                       in1=rs[:, 4, :], op0=ALU.add, op1=ALU.mult
                                       ).then_inc(RT.sem, 1)

            def softmax_of_two(m):
                dve.wait_ge(RT.sem, RT.at("egap", m))
                V.tensor_scalar(rs[:, 8, :], rs[:, 2, :], 1.0, None, ALU.add).then_inc(RT.sem, 1)

            def weight1(m):
                dve.wait_ge(RT.sem, RT.at("egap1", m))
                V.reciprocal(rs[:, 9, :], rs[:, 8, :]).then_inc(RT.sem, 1)

            def part(m):
                dve.wait_ge(RT.sem, RT.at("w1", m))
                V.tensor_tensor(rt[:, 7, :, :], rt[:, 7, :, :], per_token(rs[:, 9, :], E),
                                ALU.mult).then_inc(RT.sem, 1)

            def gates(m):
                dve.wait_ge(RT.sem, RT.at("part", m))
                V.tensor_tensor(rt[:, 8, :, :], rt[:, 7, :, :], rt[:, 5, :, :], ALU.add
                                ).then_inc(RT.sem, 1)

            gates_twice = rt[:, 8, :, :].unsqueeze(2).to_broadcast([TP, G, 2, E])

            def gates_high(m):
                dve.wait_ge(RT.sem, RT.at("gates", m))
                V.tensor_copy(gate[:, :, :, 0, :], gates_twice).then_inc(RT.sem, 1)

            def gates_low(m):
                dve.wait_ge(RT.sem, RT.at("high", m))
                V.tensor_tensor(gate[:, :, :, 1, :], gates_twice, gate[:, :, :, 0, :],
                                ALU.subtract).then_inc(RT.sem, 1)

            def step(s, slot, at_work):
                S, F, A, B_, M, N = at_work
                f, a, b, m, n = s, s - 1, s - 2, s - 3, s - 4
                t2p = bt[0:TP, 0:G * (C + 2)].rearrange("p (g c) -> p g c", g=G)
                kv = bs[:, 0:2 * (C + 1)].rearrange("p (b c) -> p b c", b=2)
                if M:
                    dve.wait_ge(CE.sem, CE.at(1, m))
                    dve.wait_ge(L2.sem, L2.at("rstd", m))
                    V.tensor_tensor(t2[:, :, :], t2[:, :, :], per_token(ln2[:, 6, :]),
                                    ALU.mult).then_inc(L2.sem, 1)
                if A:
                    if worked(a - 1):
                        dve.wait_ge(L1.sem, L1.at("low", a - 1))
                    dve.wait_ge(L1.sem, L1.at("rstd", a))
                    V.tensor_tensor(
                        t1[:, :, :].rearrange("p (b j) c -> p b j c", b=2),
                        hc[:, :, :, :].rearrange("p j b c -> p b j c"),
                        ln1[:, 2, :].rearrange("p (b j) -> p b j", b=2).unsqueeze(3)
                        .to_broadcast([TP, 2, NT, C]), ALU.mult).then_inc(L1.sem, 1)
                if N:
                    if worked(n - 2):
                        dve.wait_ge(EO.sem, EO.at("product1", n - 2))
                    dve.wait_ge(RT.sem, RT.at("turn", n))
                    V.tensor_copy(gateT[:, slot, :, :], bl[0:4 * E, 0:G * TE].rearrange(
                        "p (g t) -> p g t", g=G)[:, :, 0:TP]).then_inc(RT.sem, 1)
                if S:
                    dve.wait_ge(SET.sem, SET.at("vw", 0))
                    V.tensor_copy(stack[:, V0:V0 + C], bh[0][:, 0:C])
                    V.tensor_copy(kv_row[:, 1, :], bh[1][0:1, 0:C]).then_inc(SET.sem, 1)
                if B_:
                    dve.wait_ge(AT.sem, AT.at("t2", b))
                    V.tensor_scalar(at[:, 0, :], t2p[:, :, C], EPS_DIV, None, ALU.add
                                    ).then_inc(AT.sem, 1)
                    dve.wait_ge(AT.sem, AT.at("eps", b))
                    V.reciprocal(at[:, 1, :], at[:, 0, :]).then_inc(AT.sem, 1)
                if M:
                    if worked(m - 1):
                        dve.wait_ge(E1P.sem, E1P.at(2 * J, m - 1))
                    dve.wait_ge(L2.sem, L2.at("turn", m))
                    V.tensor_copy(l2[:, :, :], bl[:, 0:G * TE].rearrange(
                        "p (g t) -> p g t", g=G)[:, :, 0:TP]).then_inc(L2.sem, 1)
                if B_:
                    dve.wait_ge(AT.sem, AT.at("recip", b))
                    V.tensor_tensor(at[:, 2, :], t2p[:, :, C + 1], at[:, 1, :], ALU.mult
                                    ).then_inc(AT.sem, 1)
                if F:
                    tap(f, 1)
                if B_:
                    dve.wait_ge(AT.sem, AT.at("n1", b))
                    V.tensor_tensor(at[:, 3, :], at[:, 2, :], at[:, 1, :], ALU.mult
                                    ).then_inc(AT.sem, 1)
                    dve.wait_ge(AT.sem, AT.at("n2", b))
                    V.tensor_scalar(at[:, 4, :], at[:, 3, :], EPS_NORM ** 2, None, ALU.max
                                    ).then_inc(AT.sem, 1)
                if F:
                    tap(f, 2)
                    tap(f, 3)
                    tap(f, 4)
                if B_:
                    dve.wait_ge(AT.sem, AT.at("rlen", b))
                    V.tensor_tensor(at[:, 6, :], at[:, 5, :], at[:, 1, :], ALU.mult
                                    ).then_inc(AT.sem, 1)
                    dve.wait_ge(AT.sem, AT.at("scale", b))
                    V.tensor_tensor(att[:, :, :], t2p[:, :, 0:C], per_token(at[:, 6, :]), ALU.mult
                                    ).then_inc(AT.sem, 1)
                if F:
                    dve.wait_ge(BN.sem, BN.at("tap4", f))
                    V.bn_stats(stats[:, :], y[:, :]).then_inc(BN.sem, 1)
                if A:
                    dve.wait_ge(KE.sem, KE.at(3, a))
                    V.tensor_reduce(ks[:, 0, :], k_sq[:, :, :], AX, ALU.add).then_inc(KN.sem, 1)
                if N:
                    gated(n, 0)
                if A:
                    dve.wait_ge(KN.sem, KN.at("sum", a))
                    V.tensor_scalar(ks[:, 1, :], ks[:, 0, :], EPS_DIV, None, ALU.add
                                    ).then_inc(KN.sem, 1)
                if F:
                    dve.wait_ge(BN.sem, BN.at("stats", f))
                    dve.sem_inc(carrier)
                    V.bn_aggr(bn[:, 0:2], stats[:, :]).then_inc(BN.sem, 1)
                if M:
                    largest(m)
                if S:
                    dve.wait_ge(SET.sem, SET.at("bq", 0))
                    V.tensor_copy(bqc[:, :], bt[:, 0:1]).then_inc(SET.sem, 1)
                    V.tensor_reduce(row_mean[:, 0:1], stack[:, Q0:Q0 + C], AX, ALU.add, negate=True)
                    V.tensor_reduce(row_mean[:, 1:2], stack[:, K0:K0 + C], AX, ALU.add, negate=True)
                    V.tensor_reduce(row_mean[0:1, 2:3], kv_row[:, 0, :], AX, ALU.add, negate=True
                                    ).then_inc(SET.sem, 1)
                if A:
                    dve.wait_ge(KN.sem, KN.at("eps", a))
                    V.reciprocal(ks[:, 2, :], ks[:, 1, :]).then_inc(KN.sem, 1)
                if M:
                    shift(m)
                if N:
                    gated(n, 1)
                if A:
                    dve.wait_ge(KN.sem, KN.at("recip", a))
                    V.tensor_tensor(kk[:, :, 0, :], k_sq[:, :, :], per_token(ks[:, 2, :]),
                                    ALU.mult).then_inc(KN.sem, 1)
                if F:
                    dve.wait_ge(BN.sem, BN.at("mean", f))
                    V.tensor_tensor(bn[:, 2:3], bn[:, 0:1], bs[:, 0:1], ALU.subtract
                                    ).then_inc(BN.sem, 1)
                if M:
                    total(m)
                if F:
                    dve.wait_ge(BN.sem, BN.at("dev", f))
                    V.scalar_tensor_tensor(out=bn[:, 3:4], in0=bn[:, 2:3], scalar=bn[:, 2:3],
                                           in1=bn[:, 1:2], op0=ALU.mult, op1=ALU.add
                                           ).then_inc(BN.sem, 1)
                if N:
                    gated(n, 2)
                if M:
                    over_total(m)
                    marked(m, 1)
                if F:
                    dve.wait_ge(BN.sem, BN.at("var", f))
                    V.tensor_scalar(bn[:, 4:5], bs[:, 1:2], EPS_BATCH, None, ALU.add
                                    ).then_inc(BN.sem, 1)
                if M:
                    first_of(m, 1)
                if S:
                    dve.wait_ge(s_w, 16 * len(weight_loads))
                    V.tensor_scalar(b3_kept[:, :], b3[:, :], rank_in[0:4 * E, E + 1:E + 2], None,
                                    ALU.mult).then_inc(HALF.sem, 1)
                    dve.wait_ge(SET.sem, SET.at("mean", 0))
                    V.tensor_scalar(row_mean[:, 0:2], row_mean[:, 0:2], 1.0 / C, None, ALU.mult)
                    V.tensor_scalar(row_mean[0:1, 2:3], row_mean[0:1, 2:3], 1.0 / C, None,
                                    ALU.mult).then_inc(SET.sem, 1)
                if N:
                    gated(n, 3)
                if F:
                    dve.wait_ge(BN.sem, BN.at("rstd", f))
                    V.tensor_tensor(bn[:, 6:7], bn[:, 5:6], gamma, ALU.mult).then_inc(BN.sem, 1)
                    V.tensor_tensor(bn[:, 9:10], bn[:, 5:6], negative[:, 0:1], ALU.mult
                                    ).then_inc(BN.sem, 1)
                if M:
                    one_hot(m, 1)
                if F:
                    dve.wait_ge(BN.sem, BN.at("scale", f))
                    V.scalar_tensor_tensor(out=bn[:, 7:8], in0=bn[:, 2:3], scalar=bn[:, 0:1],
                                           in1=bn[:, 6:7], op0=ALU.subtract, op1=ALU.mult
                                           ).then_inc(BN.sem, 1)
                if N:
                    gated(n, 4)
                if F:
                    dve.wait_ge(BN.sem, BN.at("shift0", f))
                    V.tensor_tensor(bn[:, 8:9], beta, bn[:, 7:8], ALU.add
                                    ).then_inc(BN.sem, 1)
                if M:
                    rest(m)
                if F:
                    V.scalar_tensor_tensor(out=bn[:, 10:11], in0=bn[:, 7:8], scalar=-1.0, in1=beta,
                                           op0=ALU.mult, op1=ALU.subtract).then_inc(BN.sem, 1)
                if S:
                    dve.wait_ge(HALF.sem, HALF.at("high", 0))
                    V.scalar_tensor_tensor(out=b3_parts[:, :], in0=b3_hi[:, :],
                                           scalar=rank_in[0:4 * E, E:E + 1], in1=b3_kept[:, :],
                                           op0=ALU.mult, op1=ALU.add).then_inc(HALF.sem, 1)
                if B_:
                    hT = bx[0:TP, 0:NT * 128].rearrange("p (j b c) -> p b j c", j=NT, b=2)
                    dve.wait_ge(HT.sem, HT.at(1, b))
                    dve.wait_ge(AT.sem, AT.at("plus_v", b))
                    if worked(b - 2):
                        dve.wait_ge(YR.sem, YR.at(1, b - 2))
                    V.tensor_tensor(h2[:, slot, :, :].rearrange("p (b j) c -> p b j c", b=2),
                                    hT, att_v[:, :, :].rearrange("p (b j) c -> p b j c", b=2),
                                    ALU.add).then_inc(AT.sem, 1)
                if M:
                    second(m)
                if S:
                    dve.wait_ge(SET.sem, SET.at("scaled", 0))
                    V.tensor_scalar(stack[:, Q0 + C:Q0 + 2 * C], stack[:, Q0:Q0 + C],
                                    row_mean[:, 0:1], None, ALU.add)
                    V.tensor_scalar(stack[:, K0:K0 + C], stack[:, K0:K0 + C], row_mean[:, 1:2],
                                    None, ALU.add)
                    V.tensor_scalar(kv_row[:, 0, :], kv_row[:, 0, :], row_mean[0:1, 2:3], None,
                                    ALU.add).then_inc(SET.sem, 1)
                    dve.wait_ge(SET.sem, SET.at("centred", 0))
                    V.tensor_copy(stack[:, Q0:Q0 + C], stack[:, Q0 + C:Q0 + 2 * C])
                    for j in range(NT):
                        i = V.tensor_copy(kv_bias[0:1, j, :],
                                          kv_row[:, :, :].rearrange("p a c -> p (a c)"))
                    i.then_inc(SET.sem, 1)
                if B_:
                    dve.wait_ge(AT.sem, AT.at("h2", b))
                    for g in range(G):
                        i = V.bn_stats(st2[:, g, :], h2[:, slot, g, :])
                    i.then_inc(L2.sem, 1)
                if M:
                    below_second(m)
                if F:
                    if worked(f - 1):
                        dve.wait_ge(L1.sem, L1.at("centred", f - 1))
                    if worked(f - 1):
                        dve.wait_ge(HB.sem, HB.at(1, f - 1))
                    dve.wait_ge(BN.sem, BN.at("below", f))
                    V.scalar_tensor_tensor(out=h[:, :, :], in0=below[:, :, :],
                                           scalar=negative[:, 1:2], in1=above[:, :, :],
                                           op0=ALU.mult, op1=ALU.add).then_inc(BN.sem, 1)
                if B_:
                    dve.wait_ge(L2.sem, L2.at("stats", b))
                    V.tensor_tensor(ln2[:, 0, :], st2[:, :, 1], st2[:, :, 4], ALU.subtract
                                    ).then_inc(L2.sem, 1)
                if M:
                    marked(m, 2)
                if B_:
                    V.tensor_tensor(ln2[:, 1, :], st2[:, :, 1], st2[:, :, 4], ALU.add
                                    ).then_inc(L2.sem, 1)
                if N:
                    gated(n, 5)
                if M:
                    first_of(m, 2)
                if A:
                    dve.wait_ge(KN.sem, KN.at("kv", a))
                    V.tensor_scalar(kn[:, 0, :], kv[C:2 * C, :, C], EPS_NORM ** 2, None, ALU.max
                                    ).then_inc(KN.sem, 1)
                if B_:
                    V.tensor_tensor(ln2[:, 2, :], st2[:, :, 2], st2[:, :, 5], ALU.add
                                    ).then_inc(L2.sem, 1)
                if M:
                    one_hot(m, 2)
                    difference(m)
                if B_:
                    dve.wait_ge(L2.sem, L2.at("dm", b))
                    V.tensor_tensor(ln2[:, 3, :], ln2[:, 0, :], ln2[:, 0, :], ALU.mult
                                    ).then_inc(L2.sem, 1)
                    dve.wait_ge(L2.sem, L2.at("dm2", b))
                    V.scalar_tensor_tensor(out=ln2[:, 4, :], in0=ln2[:, 3, :], scalar=C / 4.0,
                                           in1=ln2[:, 2, :], op0=ALU.mult, op1=ALU.add
                                           ).then_inc(L2.sem, 1)
                    V.tensor_scalar(ln2[:, 7, :], ln2[:, 1, :], 0.5, None, ALU.mult
                                    ).then_inc(L2.sem, 1)
                if M:
                    softmax_of_two(m)
                if B_:
                    dve.wait_ge(L2.sem, L2.at("var", b))
                    V.tensor_scalar(ln2[:, 5, :], ln2[:, 4, :], 1.0 / C, EPS_LAYER, ALU.mult,
                                    ALU.add).then_inc(L2.sem, 1)
                if S:
                    dve.wait_ge(SET.sem, SET.at("bias", 0))
                    for j in range(NT):
                        i = V.tensor_tensor(kv_lo[:, j, :],
                                            kv_row[:, :, :].rearrange("p a c -> p (a c)"),
                                            kv_bias[0:1, j, :], ALU.subtract)
                    i.then_inc(SET.sem, 1)
                if B_:
                    if worked(b - 1):
                        dve.wait_ge(L2.sem, L2.at("low", b - 1))
                    dve.wait_ge(L2.sem, L2.at("mean", b))
                    V.tensor_tensor(t2[:, :, :], h2[:, slot, :, :], per_token(ln2[:, 7, :]),
                                    ALU.subtract).then_inc(CE.sem, 1)
                if M:
                    weight1(m)
                if F:
                    dve.wait_ge(L1.sem, L1.at("moved", f))
                    V.tensor_reduce(ln1[:, 0, :].rearrange("p (b j) -> p j b", b=2),
                                    sq1[:, :, :, :], AX, ALU.add).then_inc(L1.sem, 1)
                if M:
                    part(m)
                if F:
                    dve.wait_ge(L1.sem, L1.at("sum", f))
                    V.tensor_scalar(ln1[:, 1, :], ln1[:, 0, :], 1.0 / C, EPS_LAYER, ALU.mult,
                                    ALU.add).then_inc(L1.sem, 1)
                if M:
                    gates(m)
                if A:
                    dve.wait_ge(KN.sem, KN.at("rlen", a))
                    if worked(a - 1):
                        dve.wait_ge(AT.sem, AT.at("t2", a - 1))
                    for h_ in range(2):
                        V.tensor_scalar(kvn[0:C, h_, 0:C], kv[0:C, h_, 0:C], kn[:, 1, h_:h_ + 1],
                                        float(T) ** -0.5, ALU.mult, ALU.mult).then_inc(KN.sem, 1)
                if M:
                    gates_high(m)
                    gates_low(m)

            steps(dve, step)


def kernel(**inputs):
    import numpy as np
    import concourse.bacc as bacc
    from concourse.bass_utils import run_bass_kernel_spmd

    x = inputs["x"]
    B, TIN, C = x.shape
    w = {n.split("_", 2)[2]: np.asarray(a) for n, a in inputs.items() if n != "x"}
    E, _, H = w["expert_w1"].shape
    RH = w["router_w1"].shape[1]
    TAPS = w["w"].shape[0]
    J = E // 2
    blocks = np.kron(np.eye(2), np.ones((C, C))) / C
    pick = np.zeros((4 * E, J, 128))
    for e in range(E):
        for part in range(2):
            pick[e + part * E, e // 2, (e % 2) * C:(e % 2 + 1) * C] = 1.0
    signs = np.repeat([[1, 0], [-1, 1]], 2 * E, 0)
    signs = np.concatenate([signs, np.zeros((128 - 4 * E, 2))])
    const = {"squares": np.stack([np.eye(128), np.eye(128) - blocks, blocks], 1),
             "rank": np.concatenate([np.tile(np.arange(E, 0, -1), (128, 1)), signs], 1), "pick": pick}

    def twice(a):
        return np.concatenate([a, a], 0)

    q, k, v = np.split(w["W_qkv"], 3, 1)
    bq, bk, bv = np.split(w["b_qkv"], 3)
    w1 = w["expert_w1"].transpose(1, 0, 2).reshape(C, E * H)
    columns = [twice(w["w"].reshape(TAPS, C).T)]
    columns += [twice(a[:, None]) for a in (w["b"], w["gamma"], w["beta"], w["alpha"], w["b_out"], bq)]
    columns += [w["expert_b1"].reshape(J, 128).T, w["expert_b2"].reshape(J, 128).T]
    columns += [np.concatenate([w["router_b1"], np.zeros(128 - RH, np.float32)])[:, None]]
    w2 = np.zeros((2, H, J, 2, H), np.float32)
    for a in range(2):
        w2[a, :, :, a, :] = w["expert_w2"][a::2].transpose(1, 0, 2)
    laid = {
        "stack": twice(np.concatenate([q, q, k, v, w1, w["router_w1"]], 1)),
        "head": np.concatenate([v.T, v.T, w["W_out"], bv[:, None]], 1),
        "b_k": bk[None], "b3": twice(twice(w["expert_b3"])),
        "wr2": np.concatenate([w["router_w2"], w["router_b2"][None]], 0),
        "w3": w["expert_w3"].reshape(J, 128, C).transpose(1, 0, 2),
        "w2": w2.reshape(128, J, 128), "cols": np.concatenate(columns, 1),
    }
    nc = bacc.Bacc("TRN2", target_bir_lowering=False, num_devices=1)
    arrays = {}

    def given(name, a):
        a = np.ascontiguousarray(a)
        arrays[name] = a
        return nc.dram_tensor(name, a.shape, mybir.dt.from_np(a.dtype), kind="ExternalInput").ap()

    xs = given("x_dram", x)
    ws = {n: given(f"{n}_dram", a) for n, a in laid.items()}
    cs = {n: given(f"{n}_const", a.astype(np.float32)) for n, a in const.items()}
    out = nc.dram_tensor("out_dram", (B, TIN // 2, C), F32, kind="ExternalOutput").ap()
    audio_tower(nc, xs, ws, cs, out, E, H, RH, TAPS)
    r = run_bass_kernel_spmd(nc, [arrays], core_ids=[0])
    return r.results[0]["out_dram"]
```
